# Optimizing a Trainium2 kernel written in Bass

```python
import numpy as np
import jax
import jax.numpy as jnp

def _softmax(x, axis=-1):
    return jax.nn.softmax(x, axis=axis)

def _gelu(x):
    return jax.nn.gelu(x, approximate=True)

def _silu(x):
    return jax.nn.silu(x)

def _sigmoid(x):
    return jax.nn.sigmoid(x)

def _layernorm(x, axis=-1, eps=1e-05):
    m = jnp.mean(x, axis=axis, keepdims=True)
    v = jnp.var(x, axis=axis, keepdims=True)
    return (x - m) / jnp.sqrt(v + eps)

def _scatter_add(tgt, idx, src, axis=0):
    return tgt.at[idx].add(src)

def _segment_sum(src, seg, n):
    return jax.ops.segment_sum(src, seg, n)
kernel_name = 'mk_sandwich_d1_jaxref_r2_2f6a4d'

def setup_inputs(seed: int=0):
    np.random.seed(seed)
    _w = jnp.asarray

    def _L0_attn_setup():
        import jax, jax.numpy as jnp
        import numpy as np
        D_MODEL = 512
        D_STATE = 128
        key = jax.random.key(seed)
        ks = jax.random.split(key, 16)
        dm, ds = (D_MODEL, D_STATE)

        def lin(kw, kb, out_f, in_f):
            bound = 1.0 / np.sqrt(in_f)
            W = jax.random.uniform(kw, (out_f, in_f), jnp.float32, -bound, bound)
            b = jax.random.uniform(kb, (out_f,), jnp.float32, -bound, bound)
            return (W, b)
        x = jax.random.normal(ks[0], (8, 1024, dm), jnp.float32)
        A = jax.random.normal(ks[1], (ds, ds), jnp.float32) * 0.05
        B_w, B_b = lin(ks[2], ks[3], ds, dm)
        C_w, C_b = lin(ks[4], ks[5], dm, ds)
        D_w, D_b = lin(ks[6], ks[7], dm, dm)
        s_w1, s_b1 = lin(ks[8], ks[9], dm // 2, dm)
        s_w2, s_b2 = lin(ks[10], ks[11], ds, dm // 2)
        g_w, g_b = lin(ks[12], ks[13], dm, dm)
        return {'x': x, 'A': A, 'B_w': B_w, 'B_b': B_b, 'C_w': C_w, 'C_b': C_b, 'D_w': D_w, 'D_b': D_b, 's_w1': s_w1, 's_b1': s_b1, 's_w2': s_w2, 's_b2': s_b2, 'g_w': g_w, 'g_b': g_b}
    _L0_attn_in = _L0_attn_setup()

    def _L0_ffn_setup():
        import jax, jax.numpy as jnp
        import numpy as np
        D_MODEL = 512
        EXPERT_DIM = 256
        N_EXPERTS = 8
        TOP_K = 2

        def _sq_relu(h):
            return jnp.square(jax.nn.relu(h))
        key = jax.random.key(seed)
        ks = jax.random.split(key, 6)
        s = 0.02
        x = jax.random.normal(ks[0], (2, 1024, D_MODEL), dtype=jnp.float32)
        Ws1 = jax.random.normal(ks[1], (D_MODEL, EXPERT_DIM), dtype=jnp.float32) * s
        Ws2 = jax.random.normal(ks[2], (EXPERT_DIM, D_MODEL), dtype=jnp.float32) * s
        W1 = jax.random.normal(ks[3], (N_EXPERTS, D_MODEL, EXPERT_DIM), dtype=jnp.float32) * s
        W2 = jax.random.normal(ks[4], (N_EXPERTS, EXPERT_DIM, D_MODEL), dtype=jnp.float32) * s
        Wr = jax.random.normal(ks[5], (D_MODEL, N_EXPERTS), dtype=jnp.float32) * s
        return {'x': x, 'Ws1': Ws1, 'Ws2': Ws2, 'W1': W1, 'W2': W2, 'Wr': Wr}
    _L0_ffn_in = _L0_ffn_setup()
    _d = {'L0_attn_x': _L0_attn_in['x'], 'L0_attn_A': _L0_attn_in['A'], 'L0_attn_B_w': _L0_attn_in['B_w'], 'L0_attn_B_b': _L0_attn_in['B_b'], 'L0_attn_C_w': _L0_attn_in['C_w'], 'L0_attn_C_b': _L0_attn_in['C_b'], 'L0_attn_D_w': _L0_attn_in['D_w'], 'L0_attn_D_b': _L0_attn_in['D_b'], 'L0_attn_s_w1': _L0_attn_in['s_w1'], 'L0_attn_s_b1': _L0_attn_in['s_b1'], 'L0_attn_s_w2': _L0_attn_in['s_w2'], 'L0_attn_s_b2': _L0_attn_in['s_b2'], 'L0_attn_g_w': _L0_attn_in['g_w'], 'L0_attn_g_b': _L0_attn_in['g_b'], 'L0_ffn_Ws1': _L0_ffn_in['Ws1'], 'L0_ffn_Ws2': _L0_ffn_in['Ws2'], 'L0_ffn_W1': _L0_ffn_in['W1'], 'L0_ffn_W2': _L0_ffn_in['W2'], 'L0_ffn_Wr': _L0_ffn_in['Wr']}
    _x0 = _d['L0_attn_x']
    _d['L0_attn_x'] = jax.random.normal(jax.random.fold_in(jax.random.key(seed), 1), (8, 1024, 512), dtype=_x0.dtype)
    del _x0
    return _d

def reference(L0_attn_x, L0_attn_A, L0_attn_B_w, L0_attn_B_b, L0_attn_C_w, L0_attn_C_b, L0_attn_D_w, L0_attn_D_b, L0_attn_s_w1, L0_attn_s_b1, L0_attn_s_w2, L0_attn_s_b2, L0_attn_g_w, L0_attn_g_b, L0_ffn_Ws1, L0_ffn_Ws2, L0_ffn_W1, L0_ffn_W2, L0_ffn_Wr):

    def _L0_attn_ref(x, A, B_w, B_b, C_w, C_b, D_w, D_b, s_w1, s_b1, s_w2, s_b2, g_w, g_b):
        import jax, jax.numpy as jnp
        import numpy as np
        D_MODEL = 512
        D_STATE = 128
        s = jax.nn.sigmoid(jax.nn.silu(jnp.einsum('btd,hd->bth', x, s_w1) + s_b1) @ s_w2.T + s_b2)
        Bt = jnp.einsum('btd,sd->bts', x, B_w) + B_b
        u = Bt * s
        h0 = jnp.zeros((x.shape[0], A.shape[0]), x.dtype)

        def step(h, u_t):
            h = h @ A.T + u_t
            return (h, h)
        _, hs = jax.lax.scan(step, h0, jnp.swapaxes(u, 0, 1))
        hs = jnp.swapaxes(hs, 0, 1)
        y = jnp.einsum('bts,ds->btd', hs, C_w) + C_b + jnp.einsum('btd,ed->bte', x, D_w) + D_b
        gate = jax.nn.sigmoid(jnp.einsum('btd,ed->bte', x, g_w) + g_b)
        return y * gate

    def _L0_ffn_ref(x, Ws1, Ws2, W1, W2, Wr):
        import jax, jax.numpy as jnp
        import numpy as np
        D_MODEL = 512
        EXPERT_DIM = 256
        N_EXPERTS = 8
        TOP_K = 2

        def _sq_relu(h):
            return jnp.square(jax.nn.relu(h))
        shape = x.shape
        xf = x.reshape(-1, D_MODEL)
        out_shared = _sq_relu(xf @ Ws1) @ Ws2
        logits = xf @ Wr
        top_vals, top_idx = jax.lax.top_k(logits, TOP_K)
        rw = jax.nn.softmax(top_vals.astype(jnp.float32), axis=-1).astype(x.dtype)
        onehot = jax.nn.one_hot(top_idx, N_EXPERTS, dtype=x.dtype)
        prob = jnp.einsum('tk,tke->te', rw, onehot)
        prob = jnp.trunc(prob)
        h = _sq_relu(jnp.einsum('td,edf->tef', xf, W1))
        y = jnp.einsum('tef,efd->ted', h, W2)
        out_routed = jnp.einsum('ted,te->td', y, prob)
        return (out_shared + out_routed).reshape(shape)
    x = L0_attn_x
    x = x + _layernorm(_L0_attn_ref(_layernorm(x, axis=-1), L0_attn_A, L0_attn_B_w, L0_attn_B_b, L0_attn_C_w, L0_attn_C_b, L0_attn_D_w, L0_attn_D_b, L0_attn_s_w1, L0_attn_s_b1, L0_attn_s_w2, L0_attn_s_b2, L0_attn_g_w, L0_attn_g_b), axis=-1)
    x = x + _layernorm(_L0_ffn_ref(_layernorm(x, axis=-1), L0_ffn_Ws1, L0_ffn_Ws2, L0_ffn_W1, L0_ffn_W2, L0_ffn_Wr), axis=-1)
    return x

_drawn_inputs = setup_inputs


def setup_inputs(seed=0):
    import zlib

    import numpy as np

    out = dict(_drawn_inputs(seed))
    spreads = {}
    factors = {'L0_attn_B_b': 5.509, 'L0_attn_s_b1': 55.607, 'L0_attn_s_b2': 8.0, 'L0_attn_g_b': 6.637}
    for name, (base, spread) in spreads.items():
        noise = np.random.default_rng([zlib.crc32(name.encode()), seed]).standard_normal(out[name].shape)
        drawn = base * np.exp(spread * noise) if base else spread * noise
        out[name] = jnp.asarray(drawn.astype(out[name].dtype))
    for name, factor in factors.items():
        out[name] = (out[name] * factor).astype(out[name].dtype)
    return out
```

```python
from contextlib import ExitStack

import concourse.bass as bass
from concourse import mybir

ALU = mybir.AluOpType
ACT = mybir.ActivationFunctionType
AX = mybir.AxisListType
F32 = mybir.dt.float32
F32R = mybir.dt.float32r
I32 = mybir.dt.int32

P = 128
EPS = 1e-5


def build(nc, x, A, AT, BwT, Bb, CwT, Cb, DwT, Db, s1T, s1b, s2T, s2b, gwT, gb, Ws1, Ws2, W1, W2, Wr, eye, out):
    NB, T, D = x.shape
    NS = A.shape[0]
    NE, _, FH = W1.shape
    KD = D // P
    KF = FH // P
    L = T // P
    MS = 4
    NM = L // MS
    assert NS == P and D == 512 and FH == 256 and L == 8 and T == P * L

    x_v = x.rearrange("b (c j) d -> b c j d", j=L)
    out_v = out.rearrange("b (c j) d -> b c j d", j=L)
    x1_dram = nc.dram_tensor("x1_scratch", [NB, T, D], F32).ap()
    x1_v = x1_dram.rearrange("b (c j) d -> b c j d", j=L)

    with ExitStack() as ctx:
        def sb(name, shape, dt=F32):
            return ctx.enter_context(nc.sbuf_tensor(name, shape, dt))

        def sem(name):
            return ctx.enter_context(nc.semaphore(name))

        def pair(name, cols):
            return sb(name + "_hi", [P, cols], F32R), sb(name + "_lo", [P, cols], F32R)

        s1_w = pair("s1w", KD * FH)
        s2_w = pair("s2w", KF * NS)
        b_w = pair("bw", KD * NS)
        c_w = pair("cw", D)
        d_w = pair("dw", KD * D)
        g_w = pair("gw", KD * D)
        f1_w = pair("f1w", KD * FH)
        RC = 2 * NE
        f2_hi = sb("f2w_hi", [P, KD * RC + KF * D], F32R)
        f2_lo = sb("f2w_lo", [P, KF * D], F32R)
        ones2 = sb("ones2", [P, P], F32R)
        bias_y = sb("bias_y", [P, D], F32R)
        bias_g = sb("bias_g", [P, D], F32R)

        xin = sb("xin", [P, L, D])
        xres = sb("xres", [P, L, D])
        work = sb("work", [P, L, D])
        xT_hi = sb("xT_hi", [P, L, KD, P], F32R)
        xT_lo = sb("xT_lo", [P, L, KD, P], F32R)
        x2T_hi = sb("x2T_hi", [P, MS, KD, P], F32R)
        x2T_lo = sb("x2T_lo", [P, MS, KD, P], F32R)
        h1_hi = sb("h1_hi", [P, KF, MS * P], F32R)
        h1_lo = sb("h1_lo", [P, KF, MS * P], F32R)
        h2_hi = sb("h2_hi", [P, KF, MS * P], F32R)
        h2_lo = sb("h2_lo", [P, KF, MS * P], F32R)
        hf = sb("hf", [P, 2, MS * P])
        sg = sb("sg", [P, MS * P])
        u = sb("u", [P, L, P])
        carry = sb("carry", [P, P + 1])
        hs_hi = sb("hs_hi", [P, 2, P], F32R)
        hs_lo = sb("hs_lo", [P, 2, P], F32R)
        POW = [1, 2, 3, 4, 5, 6, 7, 8, 16, 24, 32, 64, 96, 128, 256, 384, 512]
        apt = sb("apt", [P, len(POW), P])
        ident = sb("ident", [P, P])
        comb = sb("comb", [RC, NE])
        b_col = sb("b_col", [P, 4])
        negh = sb("negh", [P, MS])
        st6 = sb("st6", [P, 4, 6])
        mv1 = sb("mv1", [P, L, 2])
        ve1 = sb("ve1", [P, L])
        rs1 = sb("rs1", [P, L])
        mvv = sb("mvv", [P, L, 2])
        rsv = sb("rsv", [P, L])
        mvx = sb("mvx", [P, L, 2])
        rsx = sb("rsx", [P, L])
        mvz = sb("mvz", [P, L, 2])
        rsz = sb("rsz", [P, L])
        nmz = sb("nmz", [P, L])
        lgt = sb("lgt", [P, MS * NE])
        mx8 = sb("mx8", [P, MS, 8])
        dif = sb("dif", [P, NB * L])
        flag = sb("flag", [P, 4])
        flag_i = sb("flag_i", [P, 1], I32)

        TR = [ctx.enter_context(nc.psum_tensor(f"TR{i}", [P, 512], F32)) for i in range(2)]
        TM = [ctx.enter_context(nc.psum_tensor(f"TM{i}", [P, 512], F32)) for i in range(3)]
        FM = [ctx.enter_context(nc.psum_tensor(f"FM{i}", [P, 512], F32)) for i in range(2)]
        SC = ctx.enter_context(nc.psum_tensor("SC", [P, 512], F32))

        BODY = dict(g_done=L, scan_done=12, y_done=L, t_done=L, w1_done=NM * KF, r_done=NM, rt_done=NM, w2_done=L,
                    gate_ok=L, hs_hi_ok=L, t_hi=L, relu_ok=NM * KF, sq_ok=NM * KF, lg_ok=NM, zn_ok=L,
                    scan_ok=12, hs_lo_ok=L, v_ok=L, v_var=L, vn_ok=L, x1_var=L, xn2_ok=L, t_lo=L, h2hi_ok=NM * KF,
                    z_var=L, z_nm=L, top_ok=NM,
                    v_rs=L, x1_ok=L, x1_rs=L, h2lo_ok=NM * KF, z_rs=L, out_ok=L,
                    xres_ld=16, x1_st0=16, x1_st1=16, out_st0=16, out_st1=16)
        PREP = dict(ft_done=L, h_done=NM * KF, b_done=NM, s_done=NM,
                    ft_hi=L, sig_ok=NM * KF, s_ok=NM,
                    l1_var=NM, xn_ok=L, ft_lo=L, h1_ok=NM * KF, h1hi_ok=NM * KF, u_ok=NM,
                    l1_rs=NM, h1lo_ok=NM * KF, xin_ld=16)
        S = {n: sem(n) for n in (*BODY, *PREP)}
        w_ld = [sem(f"w_ld{i}") for i in range(6)]
        chain = sem("dve_chain")
        pchain = sem("pool_chain")
        setup_act = sem("setup_act")
        setup_dve = sem("setup_dve")
        setup_pool = sem("setup_pool")
        pw_mm = sem("pw_mm")
        pw_cp = sem("pw_cp")
        exp_ok = sem("exp_ok")
        chain_end = sem("chain_end")
        flag_dve = sem("flag_dve")
        flag_pool = sem("flag_pool")
        flag_ok = sem("flag_ok")
        EDGE = {n: sem("routed_" + n) for n in (
            "x_in", "o_ok", "o_st", "w_in0", "w_in1", "w_free", "ws_in", "var", "rs", "xn", "tr", "xt", "lg", "d", "e",
            "pr", "h", "hr", "hr1", "y", "acc")}

        def body_at(name, b, i=0):
            k = BODY[name]
            return b * k + (k + (k if k == 16 else i + 1))

        def prep_at(name, n, i=0):
            k = PREP[name]
            return n * k + (k if k == 16 else i + 1)

        raw = {}
        xres_f = xres[:, :, :].rearrange("p a b -> p (a b)")
        work_f = work[:, :, :].rearrange("p a b -> p (a b)")
        u_f = u[:, :, :].rearrange("p a b -> p (a b)")
        raw["d"] = xres_f[:, 0:2048]
        raw["g"] = xres_f[:, 2048:4096]
        raw["s1"] = work_f[:, 0:1024]
        raw["b"] = work_f[:, 1024:1536]
        raw["c"] = work_f[:, 1536:2048]
        raw["f1"] = work_f[:, 2048:3072]
        raw["f2"] = work_f[:, 3072:4096]
        raw["s2"] = u_f[:, 0:256]
        raw["r"] = u_f[:, 256:256 + KD * NE]
        PA = u_f[:, 384:512]
        PP = [sg[:, 0:128], sg[:, 128:256]]
        brow, grow = hf[:, 0, :], hf[:, 1, :]
        BIAS_ROWS = [(0, Cb, brow), (32, Cb, brow), (64, Db, brow), (96, Db, brow), (0, gb, grow), (32, gb, grow)]

        def kt(ap, n):
            return ap.rearrange("p (k n) -> p k n", n=n)

        R_hi = f2_hi[:, 0:KD * RC].rearrange("p (k c) -> p k c", c=RC)
        F2H = f2_hi[:, KD * RC:]

        SPLITS = [("s1", s1_w[0][:, :], s1_w[1][:, :]), ("b", b_w[0][:, :], b_w[1][:, :]),
                  ("s2", s2_w[0][:, :], s2_w[1][:, :]),
                  ("g", g_w[0][:, :], g_w[1][:, :]), ("d", d_w[0][:, :], d_w[1][:, :]),
                  ("c", c_w[0][:, :], c_w[1][:, :]),
                  ("f1", f1_w[0][:, :], f1_w[1][:, :]), ("f2", F2H, f2_lo[:, :])]
        GROUP = {"s1": 0, "b": 0, "s2": 0, "r": 0, "g": 1, "d": 2, "c": 3, "f1": 3, "f2": 3}
        LOADS = {0: 9, 1: 1, 2: 1, 3: 3}

        def tm_bank(kind, j):
            return TM[({"g": 0, "y": L, "z": 2 * L}[kind] + j) % 3]

        FM_BODY = ["w00", "w01", "r0", "h00", "h01", "b0", "s0", "w10", "w11", "r1", "h10", "h11", "b1", "s1"]
        FM_LAST = ["w00", "w01", "r0", "w10", "w11", "r1"]
        FM_PREP = ["h00", "h01", "b0", "s0", "h10", "h11", "b1", "s1"]
        TR_BODY = ["t0", "t1", "t2", "f0", "t3", "f1", "f2", "f3", "t4", "t5", "t6", "f4", "t7", "f5", "f6", "f7"]
        TR_LAST = [f"t{j}" for j in range(L)]
        TR_PREP = [f"f{j}" for j in range(L)]
        HF_BODY = ["w00", "w01", "r0", "h00", "h01", "w10", "w11", "r1", "h10", "h11"]
        HF_LAST = ["w00", "w01", "r0", "w10", "w11", "r1"]
        HF_PREP = ["h00", "h01", "h10", "h11"]

        def ring(order, before, name, size=2):
            i = order.index(name)
            if i >= size:
                return i % size, order[i - size], 0
            if before is None:
                return i % size, None, 0
            return i % size, before[len(before) - size + i], 1

        class Mode:
            def __init__(self, fm, tr, hfo, before):
                self.fm, self.tr, self.hf = fm, tr, hfo
                self.bfm, self.btr, self.bhf = before

            def fm_slot(self, name):
                return ring(self.fm, self.bfm, name)

            def tr_slot(self, name):
                return ring(self.tr, self.btr, name)

            def hf_slot(self, name):
                return ring(self.hf, self.bhf, name)

        PREPARE = Mode(FM_PREP, TR_PREP, HF_PREP, (None, None, None))
        assert FM_BODY[-2:] == FM_PREP[-2:] and TR_BODY[-2:] == TR_PREP[-2:] and HF_BODY[-2:] == HF_PREP[-2:]
        LOOP = Mode(FM_BODY, TR_BODY, HF_BODY, (FM_BODY, TR_BODY, HF_BODY))
        LAST = Mode(FM_LAST, TR_LAST, HF_LAST, (FM_BODY, TR_BODY, HF_BODY))

        def wait_fm_free(eng, mode, name, b, n):
            _, prev, back = mode.fm_slot(name)
            if prev is None:
                return
            m = int(prev[1])
            if prev[0] == "w":
                eng.wait_ge(S["relu_ok"], body_at("relu_ok", b - back, KF * m + int(prev[2])))
            elif prev[0] == "r":
                eng.wait_ge(S["lg_ok"], body_at("lg_ok", b - back, m))
            elif prev[0] == "h":
                eng.wait_ge(S["h1_ok"], prep_at("h1_ok", n - back, KF * m + int(prev[2])))
            elif prev[0] == "b":
                eng.wait_ge(S["u_ok"], prep_at("u_ok", n - back, m))
            else:
                eng.wait_ge(S["s_ok"], prep_at("s_ok", n - back, m))

        def wait_tr_free(eng, mode, name, b, n):
            _, prev, back = mode.tr_slot(name)
            if prev is None:
                return
            if prev[0] == "t":
                eng.wait_ge(S["t_lo"], body_at("t_lo", b - back, int(prev[1])))
            else:
                eng.wait_ge(S["ft_lo"], prep_at("ft_lo", n - back, int(prev[1])))

        def wait_hf_free(eng, mode, name, b, n):
            _, prev, back = mode.hf_slot(name)
            if prev is None:
                return
            m = int(prev[1])
            if prev[0] == "w":
                eng.wait_ge(S["h2lo_ok"], body_at("h2lo_ok", b - back, KF * m + int(prev[2])))
            elif prev[0] == "r":
                eng.wait_ge(S["rt_done"], body_at("rt_done", b - back, m))
            else:
                eng.wait_ge(S["h1lo_ok"], prep_at("h1lo_ok", n - back, KF * m + int(prev[2])))

        NT = NB * L
        q_x1, q_xn, q_acc, q_o = (work[:, i, :] for i in range(4))
        q_xT = work[:, 4, :].rearrange("p (k n) -> p k n", n=P)
        q_h = [work[:, 5, i * FH:(i + 1) * FH].rearrange("p (f n) -> p f n", n=P) for i in range(2)]
        q_small = work[:, 6, :]
        q_mv, q_rs, q_d = q_small[:, 0:2], q_small[:, 2:3], q_small[:, 3:4]
        q_lg, q_mx, q_pr = q_small[:, 8:16], q_small[:, 16:24], q_small[:, 24:24 + NE]
        q_wr = xres[:, 0, 0:KD * NE].rearrange("p (k n) -> p k n", n=NE)

        def rows(t, i):
            return t[:, i:i + 2, :].rearrange("p a b -> p (a b)")

        q_w1 = [rows(xin, 0).rearrange("p (k n) -> p k n", n=FH), rows(xin, 4).rearrange("p (k n) -> p k n", n=FH)]
        q_w2 = [rows(xin, 2).rearrange("p (k n) -> p k n", n=D), rows(xin, 6).rearrange("p (k n) -> p k n", n=D)]
        q_s1 = rows(xres, 2).rearrange("p (k n) -> p k n", n=FH)
        q_s2 = rows(xres, 4).rearrange("p (k n) -> p k n", n=D)
        x1_t = x1_dram.rearrange("b t d -> (b t) d")
        out_t = out.rearrange("b t d -> (b t) d")

        def take(eng, name, n=1):
            eng.wait_ge(EDGE[name], n)
            eng.sem_inc(EDGE[name], -n)

        def if_routed(eng):
            eng.wait_ge(flag_ok, 1)
            return eng.If(eng.value_load(flag_i[0:1, 0:1], min_val=0, max_val=1) > 0)

        block = ctx.enter_context(nc.Block())

        def credits(eng, names):
            for name in names:
                eng.sem_inc(S[name], BODY[name])

        @block.sync
        def _(eng):
            credits(eng, ["xres_ld", "x1_st0", "x1_st1", "out_st0", "out_st1"])
            eng.dma_start(xin[:, :, :], x_v[0]).then_inc(S["xin_ld"], 16)
            eng.dma_start(kt(raw["s1"], FH), s1T.rearrange("(k p) n -> p k n", p=P)).then_inc(w_ld[0], 16)
            eng.dma_start(kt(raw["b"], NS), BwT.rearrange("(k p) n -> p k n", p=P)).then_inc(w_ld[0], 16)
            eng.dma_start(kt(raw["s2"], NS), s2T.rearrange("(k p) n -> p k n", p=P)).then_inc(w_ld[0], 16)
            eng.dma_start(kt(raw["r"], NE), Wr.rearrange("(k p) n -> p k n", p=P)).then_inc(w_ld[0], 16)
            with nc.allow_non_contiguous_dma(reason="bias columns"):
                eng.dma_start(b_col[:, 0:2], s1b.rearrange("(k p) -> p k", p=P)).then_inc(w_ld[0], 16)
                eng.dma_start(b_col[:, 2:3], s2b.rearrange("(k p) -> p k", p=P)).then_inc(w_ld[0], 16)
                eng.dma_start(b_col[:, 3:4], Bb.rearrange("(k p) -> p k", p=P)).then_inc(w_ld[0], 16)
            eng.dma_start(ident[:, :], eye).then_inc(w_ld[0], 16)
            eng.dma_start(PA, A).then_inc(w_ld[0], 16)
            eng.dma_start(apt[:, 0, :], AT).then_inc(w_ld[5], 16)
            eng.dma_start(kt(raw["g"], D), gwT.rearrange("(k p) n -> p k n", p=P)).then_inc(w_ld[1], 16)
            for row, src, dst in BIAS_ROWS:
                eng.dma_start(dst[row:row + 1, :], src[None, :]).then_inc(w_ld[4], 16)
            eng.dma_start(comb[0:NE, :], eye[0:NE, 0:NE]).then_inc(w_ld[4], 16)
            eng.dma_start(comb[NE:RC, :], eye[0:NE, 0:NE]).then_inc(w_ld[4], 16)
            eng.dma_start(kt(raw["d"], D), DwT.rearrange("(k p) n -> p k n", p=P)).then_inc(w_ld[2], 16)
            eng.dma_start(raw["c"], CwT).then_inc(w_ld[3], 16)
            eng.dma_start(kt(raw["f1"], FH), Ws1.rearrange("(k p) n -> p k n", p=P)).then_inc(w_ld[3], 16)
            eng.dma_start(kt(raw["f2"], D), Ws2.rearrange("(k p) n -> p k n", p=P)).then_inc(w_ld[3], 16)
            eng.wait_ge(setup_act, 8)
            eng.wait_ge(setup_dve, 8)

            def batch(b, last):
                if not last:
                    eng.wait_ge(S["ft_done"], prep_at("ft_done", b, L - 1))
                    eng.dma_start(xin[:, :, :], x_v[b + 1]).then_inc(S["xin_ld"], 16)
                eng.wait_ge(S["out_ok"], body_at("out_ok", b - 1, L - 1))
                eng.wait_ge(S["x1_st1"], body_at("x1_st1", b - 1))
                eng.wait_ge(S["x1_st0"], body_at("x1_st0", b - 1))
                eng.dma_start(xres[:, :, :], x_v[b]).then_inc(S["xres_ld"], 16)
                for m in range(NM):
                    js = slice(m * MS, (m + 1) * MS)
                    eng.wait_ge(S["x1_ok"], body_at("x1_ok", b, m * MS + MS - 1))
                    eng.dma_start(x1_v[b][:, js, :], xres[:, js, :]).then_inc(S[f"x1_st{m}"], 16)
                for m in range(NM):
                    js = slice(m * MS, (m + 1) * MS)
                    eng.wait_ge(S["out_ok"], body_at("out_ok", b, m * MS + MS - 1))
                    eng.dma_start(out_v[b][:, js, :], work[:, js, :]).then_inc(S[f"out_st{m}"], 16)

            with eng.Fori(0, NB - 1) as b:
                batch(b, False)
            batch(NB - 1, True)
            for m in range(NM):
                eng.wait_ge(S[f"out_st{m}"], body_at(f"out_st{m}", NB - 1))
                eng.wait_ge(S[f"x1_st{m}"], body_at(f"x1_st{m}", NB - 1))

            with if_routed(eng):
                eng.dma_start(q_s1, Ws1.rearrange("(k p) n -> p k n", p=P)).then_inc(EDGE["ws_in"], 16)
                eng.dma_start(q_s2, Ws2.rearrange("(k p) n -> p k n", p=P)).then_inc(EDGE["ws_in"], 16)
                eng.dma_start(q_wr, Wr.rearrange("(k p) n -> p k n", p=P)).then_inc(EDGE["ws_in"], 16)
                eng.sem_inc(EDGE["w_free"], 2)
                with eng.Fori(0, NT) as t:
                    eng.dma_start(q_x1, x1_t[bass.ts(t, P), :]).then_inc(EDGE["x_in"], 16)
                    with eng.Fori(0, NE // 2) as e:
                        for s in range(2):
                            take(eng, "w_free")
                            eng.dma_start(q_w1[s], W1[e * 2 + s].rearrange("(k p) n -> p k n", p=P))\
                               .then_inc(EDGE[f"w_in{s}"], 16)
                            eng.dma_start(q_w2[s], W2[e * 2 + s].rearrange("(k p) n -> p k n", p=P))\
                               .then_inc(EDGE[f"w_in{s}"], 16)
                    take(eng, "o_ok")
                    eng.dma_start(out_t[bass.ts(t, P), :], q_o).then_inc(EDGE["o_st"], 16)
                    take(eng, "o_st", 16)

        @block.tensor
        def _(eng):
            credits(eng, [n for n in BODY if n.endswith("_done")])

            def mm3(ps, lhs, rhs, first, last):
                eng.matmul(ps, lhs[0], rhs[0], start=first, stop=False)
                eng.matmul(ps, lhs[0], rhs[1], start=False, stop=False)
                return eng.matmul(ps, lhs[1], rhs[0], start=False, stop=last)

            eng.wait_ge(w_ld[0], 16 * LOADS[0])
            eng.wait_ge(w_ld[5], 16)
            step = 0
            pcur, n = PA, 1
            idx = {k: i for i, k in enumerate(POW)}

            def power(lhsT, rhs):
                nonlocal step
                if step:
                    eng.wait_ge(pw_cp, step)
                eng.matmul(SC[:, 0:P], lhsT, rhs, start=True, stop=True).then_inc(pw_mm, 1)
                step += 1

            k = 1
            while k < POW[-1]:
                ptk = apt[:, idx[k], :]
                if 2 * k < POW[-1]:
                    power(ptk, pcur)
                power(pcur, ptk)
                if k == 1:
                    power(PA, apt[:, idx[2], :])
                if k == 2:
                    for q in (4, 5, 6):
                        power(PA, apt[:, idx[q], :])
                if 3 * k in (24, 96, 384):
                    power(pcur, apt[:, idx[2 * k], :])
                if 2 * k < POW[-1]:
                    pcur = PP[(k.bit_length() - 1) % 2]
                k *= 2
            eng.wait_ge(pw_cp, step)

            def scan_step(b, i):
                if i == 0:
                    eng.wait_ge(S["u_ok"], prep_at("u_ok", b, NM - 1))
                    eng.wait_ge(S["top_ok"], body_at("top_ok", b - 1, NM - 1))
                else:
                    eng.wait_ge(S["scan_ok"], body_at("scan_ok", b, i - 1))
                if i == 0:
                    for j in range(L - 1):
                        m = eng.matmul(SC[:, 0:P], apt[:, idx[L - 1 - j], :], u[:, j, :], start=(j == 0), stop=(j == L - 2))
                elif i <= 4:
                    s = 4 ** (i - 1)
                    reps = [r for r in (1, 2, 3) if r * s < P]
                    for r in reps:
                        m = eng.matmul(SC[:, r * s:P], apt[:, idx[L * s * r], :], carry[:, 1:1 + P - r * s],
                                       start=(r == 1), stop=(r == reps[-1]))
                else:
                    j = i - 5
                    prev = carry[:, 0:P] if j == 0 else u[:, j - 1, :]
                    m = eng.matmul(SC[:, 0:P], apt[:, 0, :], prev, start=True, stop=True)
                m.then_inc(S["scan_done"], 1)

            def G(b, j):
                if j < 3:
                    eng.wait_ge(S["zn_ok"], body_at("zn_ok", b - 1, L - 3 + j))
                else:
                    eng.wait_ge(S["gate_ok"], body_at("gate_ok", b, j - 3))
                ps = tm_bank("g", j)[:, :]
                eng.matmul(ps, ones2[:, :], bias_g[:, :], start=True, stop=False)
                for k in range(KD):
                    m = mm3(ps, (xT_hi[:, j, k, :], xT_lo[:, j, k, :]),
                            [w[:, k * D:(k + 1) * D] for w in g_w], False, k == KD - 1)
                    if k == 1 and 2 <= 2 * j < 2 + 12:
                        scan_step(b, 2 * j - 2)
                m.then_inc(S["g_done"], 1)
                if 2 <= 2 * j + 1 < 2 + 12:
                    scan_step(b, 2 * j - 1)

            def Y(b, j):
                if j < 3:
                    eng.wait_ge(S["gate_ok"], body_at("gate_ok", b, L - 3 + j))
                else:
                    eng.wait_ge(S["v_ok"], body_at("v_ok", b, j - 3))
                ps = tm_bank("y", j)[:, :]
                eng.matmul(ps, ones2[:, :], bias_y[:, :], start=True, stop=False)
                for k in range(KD):
                    mm3(ps, (xT_hi[:, j, k, :], xT_lo[:, j, k, :]),
                        [w[:, k * D:(k + 1) * D] for w in d_w], False, False)
                eng.wait_ge(S["hs_hi_ok"], body_at("hs_hi_ok", b, j))
                eng.wait_ge(S["hs_lo_ok"], body_at("hs_lo_ok", b, j))
                mm3(ps, (hs_hi[:, j % 2, :], hs_lo[:, j % 2, :]), [w[:, :] for w in c_w], False, True)\
                    .then_inc(S["y_done"], 1)

            def transposes(bank, src):
                for k in range(KD):
                    m = eng.transpose(bank[:, k * P:(k + 1) * P], src[:, k * P:(k + 1) * P], ident[:, :])
                return m

            def T2(mode, b, n, j):
                wait_tr_free(eng, mode, f"t{j}", b, n)
                eng.wait_ge(S["xn2_ok"], body_at("xn2_ok", b, j))
                transposes(TR[mode.tr_slot(f"t{j}")[0]], work[:, j, :]).then_inc(S["t_done"], 1)

            def FT(mode, b, n, j):
                wait_tr_free(eng, mode, f"f{j}", b, n)
                eng.wait_ge(S["xn_ok"], prep_at("xn_ok", n, j))
                transposes(TR[mode.tr_slot(f"f{j}")[0]], xin[:, j, :]).then_inc(S["ft_done"], 1)

            def W1s(mode, b, n, m):
                last = m * MS + MS - 1
                eng.wait_ge(S["t_hi"], body_at("t_hi", b, last))
                eng.wait_ge(S["t_lo"], body_at("t_lo", b, last))
                for f in range(KF):
                    wait_fm_free(eng, mode, f"w{m}{f}", b, n)
                    ps = FM[mode.fm_slot(f"w{m}{f}")[0]][:, :]
                    for k in range(KD):
                        o = k * FH + f * P
                        r = mm3(ps, [w[:, o:o + P] for w in f1_w], (x2T_hi[:, :, k, :], x2T_lo[:, :, k, :]),
                                k == 0, k == KD - 1)
                    r.then_inc(S["w1_done"], 1)

            def R(mode, b, n, m):
                wait_fm_free(eng, mode, f"r{m}", b, n)
                ps = FM[mode.fm_slot(f"r{m}")[0]][:, :]
                for k in range(KD):
                    w = f2_hi[:, k * RC:k * RC + P]
                    eng.matmul(ps, w, x2T_hi[:, :, k, :], start=(k == 0), stop=False)
                    r = eng.matmul(ps, w, x2T_lo[:, :, k, :], start=False, stop=(k == KD - 1))
                r.then_inc(S["r_done"], 1)

            def RT(mode, b, n, m):
                eng.wait_ge(S["lg_ok"], body_at("lg_ok", b, m))
                if m == 0:
                    eng.wait_ge(S["scan_ok"], body_at("scan_ok", b, 11))
                else:
                    eng.wait_ge(S["top_ok"], body_at("top_ok", b, m - 1))
                lg = hf[0:RC, mode.hf_slot(f"r{m}")[0], :]
                for s in range(MS):
                    r = eng.matmul(SC[:, s * NE:(s + 1) * NE], lg[:, s * P:(s + 1) * P], comb[:, :],
                                   start=True, stop=True)
                r.then_inc(S["rt_done"], 1)

            def W2s(b, j):
                m, s = divmod(j, MS)
                if j % MS == 0:
                    eng.wait_ge(S["h2hi_ok"], body_at("h2hi_ok", b, KF * m + KF - 1))
                    eng.wait_ge(S["h2lo_ok"], body_at("h2lo_ok", b, KF * m + KF - 1))
                if j < 3:
                    eng.wait_ge(S["v_ok"], body_at("v_ok", b, L - 3 + j))
                else:
                    eng.wait_ge(S["zn_ok"], body_at("zn_ok", b, j - 3))
                ps = tm_bank("z", j)[:, :]
                for f in range(KF):
                    c = slice(s * P, (s + 1) * P)
                    r = mm3(ps, (h2_hi[:, f, c], h2_lo[:, f, c]),
                            (F2H[:, f * D:(f + 1) * D], f2_lo[:, f * D:(f + 1) * D]), f == 0, f == KF - 1)
                r.then_inc(S["w2_done"], 1)

            def H(mode, b, n, m):
                last = m * MS + MS - 1
                eng.wait_ge(S["ft_hi"], prep_at("ft_hi", n, last))
                eng.wait_ge(S["ft_lo"], prep_at("ft_lo", n, last))
                js = slice(m * MS, (m + 1) * MS)
                for f in range(KF):
                    wait_fm_free(eng, mode, f"h{m}{f}", b, n)
                    ps = FM[mode.fm_slot(f"h{m}{f}")[0]][:, :]
                    for k in range(KD):
                        o = k * FH + f * P
                        r = mm3(ps, [w[:, o:o + P] for w in s1_w], (xT_hi[:, js, k, :], xT_lo[:, js, k, :]),
                                k == 0, k == KD - 1)
                    r.then_inc(S["h_done"], 1)

            def B(mode, b, n, m):
                js = slice(m * MS, (m + 1) * MS)
                wait_fm_free(eng, mode, f"b{m}", b, n)
                ps = FM[mode.fm_slot(f"b{m}")[0]][:, :]
                for k in range(KD):
                    r = mm3(ps, [w[:, k * NS:(k + 1) * NS] for w in b_w], (xT_hi[:, js, k, :], xT_lo[:, js, k, :]),
                            k == 0, k == KD - 1)
                r.then_inc(S["b_done"], 1)

            def SG(mode, b, n, m):
                wait_fm_free(eng, mode, f"s{m}", b, n)
                eng.wait_ge(S["h1hi_ok"], prep_at("h1hi_ok", n, KF * m + KF - 1))
                eng.wait_ge(S["h1lo_ok"], prep_at("h1lo_ok", n, KF * m + KF - 1))
                ps = FM[mode.fm_slot(f"s{m}")[0]][:, :]
                for f in range(KF):
                    r = mm3(ps, [w[:, f * NS:(f + 1) * NS] for w in s2_w], (h1_hi[:, f, :], h1_lo[:, f, :]),
                            f == 0, f == KF - 1)
                r.then_inc(S["s_done"], 1)

            def batch(mode, b):
                n = b + 1
                prep = mode is LOOP
                a = (mode, b, n)
                for j in range(L):
                    G(b, j)
                Y(b, 0)
                Y(b, 1)
                Y(b, 2)
                T2(*a, 0)
                Y(b, 3)
                T2(*a, 1)
                Y(b, 4)
                T2(*a, 2)
                if prep:
                    FT(*a, 0)
                Y(b, 5)
                T2(*a, 3)
                if prep:
                    FT(*a, 1)
                Y(b, 6)
                if prep:
                    FT(*a, 2)
                W1s(*a, 0)
                if prep:
                    FT(*a, 3)
                R(*a, 0)
                Y(b, 7)
                T2(*a, 4)
                RT(*a, 0)
                if prep:
                    H(*a, 0)
                T2(*a, 5)
                W2s(b, 0)
                W2s(b, 1)
                if prep:
                    B(*a, 0)
                T2(*a, 6)
                W2s(b, 2)
                W2s(b, 3)
                if prep:
                    SG(*a, 0)
                    FT(*a, 4)
                T2(*a, 7)
                if prep:
                    FT(*a, 5)
                    FT(*a, 6)
                    FT(*a, 7)
                W1s(*a, 1)
                R(*a, 1)
                if prep:
                    H(*a, 1)
                RT(*a, 1)
                W2s(b, 4)
                W2s(b, 5)
                if prep:
                    B(*a, 1)
                W2s(b, 6)
                W2s(b, 7)
                if prep:
                    SG(*a, 1)

            eng.wait_ge(setup_act, 9)
            eng.wait_ge(setup_dve, 11)
            a = (PREPARE, 0, 0)
            for m in range(NM):
                for j in range(m * MS, (m + 1) * MS):
                    FT(*a, j)
                H(*a, m)
                B(*a, m)
                SG(*a, m)
            with eng.Fori(0, NB - 1) as b:
                batch(LOOP, b)
            batch(LAST, NB - 1)

            def routed_ffn(w1, w2):
                for f in range(KF):
                    for k in range(KD):
                        r = eng.matmul(TM[0][:, f * P:(f + 1) * P], w1[:, k, f * P:(f + 1) * P], q_xT[:, k, :],
                                       start=(k == 0), stop=(k == KD - 1))
                r.then_inc(EDGE["h"], 1)
                take(eng, "hr")
                for f in range(KF):
                    r = eng.matmul(TM[1][:, :], q_h[1][:, f, :], w2[:, f, :], start=(f == 0), stop=(f == KF - 1))
                r.then_inc(EDGE["y"], 1)
                take(eng, "acc")

            with if_routed(eng):
                take(eng, "ws_in", 48)
                with eng.Fori(0, NT) as t:
                    take(eng, "xn")
                    transposes(TR[0], q_xn).then_inc(EDGE["tr"], 1)
                    take(eng, "xt")
                    for k in range(KD):
                        r = eng.matmul(SC[:, 0:NE], q_xT[:, k, :], q_wr[:, k, :], start=(k == 0), stop=(k == KD - 1))
                    r.then_inc(EDGE["lg"], 1)
                    take(eng, "pr")
                    routed_ffn(q_s1, q_s2)
                    with eng.Fori(0, NE // 2) as e:
                        for s in range(2):
                            take(eng, f"w_in{s}", 32)
                            routed_ffn(q_w1[s], q_w2[s])
                            eng.sem_inc(EDGE["w_free"], 1)

        @block.scalar
        def _(eng):
            credits(eng, ["gate_ok", "hs_hi_ok", "t_hi", "relu_ok", "sq_ok", "lg_ok", "zn_ok"])
            for i, (name, hi, lo) in enumerate(SPLITS):
                g = GROUP[name]
                eng.wait_ge(w_ld[g], 16 * LOADS[g])
                eng.activation(hi, raw[name], ACT.Copy).then_inc(setup_act, 1)
            eng.activation(R_hi[:, :, 0:NE], kt(raw["r"], NE), ACT.Copy).then_inc(setup_act, 1)

            def gate(b, j):
                eng.wait_ge(S["g_done"], body_at("g_done", b, j))
                if j % MS == 0:
                    m = j // MS
                    eng.wait_ge(S[f"out_st{m}"], body_at(f"out_st{m}", b - 1))
                eng.activation(work[:, j, :], tm_bank("g", j)[:, :], ACT.Sigmoid).then_inc(S["gate_ok"], 1)

            def hs(b, j):
                if j < L - 1:
                    eng.wait_ge(S["scan_ok"], body_at("scan_ok", b, 5 + j))
                if j >= 2:
                    eng.wait_ge(S["y_done"], body_at("y_done", b, j - 2))
                src = u[:, j, :] if j < L - 1 else carry[:, 1:P + 1]
                eng.activation(hs_hi[:, j % 2, :], src, ACT.Copy).then_inc(S["hs_hi_ok"], 1)

            def t_hi(mode, b, n, j):
                eng.wait_ge(S["t_done"], body_at("t_done", b, j))
                if j % MS == 0:
                    if j:
                        eng.wait_ge(S["r_done"], body_at("r_done", b, j // MS - 1))
                    else:
                        eng.wait_ge(S["r_done"], body_at("r_done", b - 1, NM - 1))
                bank = TR[mode.tr_slot(f"t{j}")[0]]
                eng.activation(x2T_hi[:, j % MS, :, :], bank[:, :].rearrange("p (k n) -> p k n", n=P), ACT.Copy)\
                   .then_inc(S["t_hi"], 1)

            def ft_hi(mode, b, n, j):
                eng.wait_ge(S["ft_done"], prep_at("ft_done", n, j))
                if mode is not PREPARE:
                    eng.wait_ge(S["y_done"], body_at("y_done", b, j))
                bank = TR[mode.tr_slot(f"f{j}")[0]]
                eng.activation(xT_hi[:, j, :, :], bank[:, :].rearrange("p (k n) -> p k n", n=P), ACT.Copy)\
                   .then_inc(S["ft_hi"], 1)

            def hidden(mode, b, n, m, f):
                i = KF * m + f
                name = f"w{m}{f}"
                eng.wait_ge(S["w1_done"], body_at("w1_done", b, i))
                wait_hf_free(eng, mode, name, b, n)
                r = hf[:, mode.hf_slot(name)[0], :]
                eng.activation(r, FM[mode.fm_slot(name)[0]][:, :], ACT.Relu).then_inc(S["relu_ok"], 1)
                eng.wait_ge(S["relu_ok"], body_at("relu_ok", b, i))
                eng.activation(r, r, ACT.Square).then_inc(S["sq_ok"], 1)

            def lg(mode, b, n, m):
                eng.wait_ge(S["r_done"], body_at("r_done", b, m))
                wait_hf_free(eng, mode, f"r{m}", b, n)
                eng.activation(hf[0:RC, mode.hf_slot(f"r{m}")[0], :], FM[mode.fm_slot(f"r{m}")[0]][0:RC, :],
                               ACT.Copy).then_inc(S["lg_ok"], 1)

            def sig(mode, b, n, m, f):
                name = f"h{m}{f}"
                eng.wait_ge(S["h_done"], prep_at("h_done", n, KF * m + f))
                wait_hf_free(eng, mode, name, b, n)
                eng.activation(hf[:, mode.hf_slot(name)[0], :], FM[mode.fm_slot(name)[0]][:, :], ACT.Sigmoid,
                               bias=b_col[:, f:f + 1]).then_inc(S["sig_ok"], 1)

            def s_gate(mode, b, n, m):
                eng.wait_ge(S["s_done"], prep_at("s_done", n, m))
                if m or mode is not PREPARE:
                    eng.wait_ge(S["u_ok"], prep_at("u_ok", n if m else n - 1, (m - 1) % NM))
                eng.activation(sg[:, :], FM[mode.fm_slot(f"s{m}")[0]][:, :], ACT.Sigmoid,
                               bias=b_col[:, 2:3]).then_inc(S["s_ok"], 1)

            def zn(b, j):
                eng.wait_ge(S["z_nm"], body_at("z_nm", b, j))
                eng.activation(work[:, j, :], tm_bank("z", j)[:, :], ACT.Identity, bias=nmz[:, j:j + 1],
                               scale=rsz[:, j:j + 1]).then_inc(S["zn_ok"], 1)

            def batch(mode, b):
                n = b + 1
                prep = mode is LOOP
                a = (mode, b, n)
                for j in range(L):
                    gate(b, j)
                hs(b, 0)
                hs(b, 1)
                hs(b, 2)
                hs(b, 3)
                hs(b, 4)
                t_hi(*a, 0)
                hs(b, 5)
                t_hi(*a, 1)
                hs(b, 6)
                t_hi(*a, 2)
                if prep:
                    ft_hi(*a, 0)
                hs(b, 7)
                t_hi(*a, 3)
                if prep:
                    ft_hi(*a, 1)
                    ft_hi(*a, 2)
                hidden(*a, 0, 0)
                hidden(*a, 0, 1)
                if prep:
                    ft_hi(*a, 3)
                lg(*a, 0)
                t_hi(*a, 4)
                if prep:
                    sig(*a, 0, 0)
                    sig(*a, 0, 1)
                t_hi(*a, 5)
                zn(b, 0)
                zn(b, 1)
                t_hi(*a, 6)
                zn(b, 2)
                zn(b, 3)
                if prep:
                    s_gate(*a, 0)
                    ft_hi(*a, 4)
                t_hi(*a, 7)
                if prep:
                    ft_hi(*a, 5)
                    ft_hi(*a, 6)
                    ft_hi(*a, 7)
                hidden(*a, 1, 0)
                hidden(*a, 1, 1)
                lg(*a, 1)
                if prep:
                    sig(*a, 1, 0)
                    sig(*a, 1, 1)
                zn(b, 4)
                zn(b, 5)
                zn(b, 6)
                zn(b, 7)
                if prep:
                    s_gate(*a, 1)

            eng.wait_ge(setup_dve, 11)
            a = (PREPARE, 0, 0)
            for m in range(NM):
                for j in range(m * MS, (m + 1) * MS):
                    ft_hi(*a, j)
                for f in range(KF):
                    sig(*a, m, f)
                s_gate(*a, m)
            with eng.Fori(0, NB - 1) as b:
                batch(LOOP, b)
            batch(LAST, NB - 1)
            eng.wait_ge(S["top_ok"], body_at("top_ok", NB - 1, NM - 1))
            eng.wait_ge(chain_end, 1)
            eng.activation(dif[:, :], dif[:, :], ACT.Exp).then_inc(exp_ok, 1)

            def routed_ffn():
                take(eng, "h")
                h = TM[0][:, 0:FH].rearrange("p (f n) -> p f n", n=P)
                eng.activation(q_h[0], h, ACT.Relu).then_inc(EDGE["hr1"], 1)
                take(eng, "hr1")
                eng.activation(q_h[1], q_h[0], ACT.Square).then_inc(EDGE["hr"], 1)

            with if_routed(eng):
                with eng.Fori(0, NT) as t:
                    take(eng, "tr")
                    eng.activation(q_xT, TR[0][:, :].rearrange("p (k n) -> p k n", n=P), ACT.Copy).then_inc(EDGE["xt"], 1)
                    take(eng, "d")
                    eng.activation(q_d, q_d, ACT.Exp).then_inc(EDGE["e"], 1)
                    routed_ffn()
                    with eng.Fori(0, NE) as e:
                        routed_ffn()

        @block.vector
        def _(eng):
            credits(eng, ["scan_ok", "hs_lo_ok", "v_ok", "v_var", "vn_ok", "x1_var", "xn2_ok", "t_lo", "h2hi_ok",
                          "z_var", "z_nm", "top_ok"])
            def link(ins):
                ins.then_inc(chain, 1)
                eng.wait_ge(chain, 1)
                eng.sem_inc(chain, -1)

            def stats(src, i, mv):
                link(eng.bn_stats(st6[:, i, :], src))
                link(eng.bn_aggr(mv, st6[:, i, :]))

            def ln1_stats(n, j):
                if j == 0:
                    eng.wait_ge(S["xin_ld"], prep_at("xin_ld", n))
                stats(xin[:, j, :], 0, mv1[:, j, :])
                if j % MS == MS - 1:
                    m = j // MS
                    js = slice(m * MS, (m + 1) * MS)
                    eng.tensor_scalar(ve1[:, js], mv1[:, js, 1], EPS, None, ALU.add).then_inc(S["l1_var"], 1)

            def ln1_norm(n, j):
                eng.wait_ge(S["l1_rs"], prep_at("l1_rs", n, j // MS))
                eng.tensor_scalar(xin[:, j, :], xin[:, j, :], mv1[:, j, 0:1], rs1[:, j:j + 1],
                                  ALU.subtract, ALU.mult).then_inc(S["xn_ok"], 1)

            def scan_add(b, i):
                eng.wait_ge(S["scan_done"], body_at("scan_done", b, i))
                if i == 0:
                    eng.wait_ge(S["hs_hi_ok"], body_at("hs_hi_ok", b - 1, L - 1))
                    r = eng.tensor_tensor(carry[:, 1:P + 1], SC[:, 0:P], u[:, L - 1, :], ALU.add)
                elif i <= 4:
                    s = 4 ** (i - 1)
                    r = eng.tensor_tensor(carry[:, 1 + s:P + 1], SC[:, s:P], carry[:, 1 + s:P + 1], ALU.add)
                else:
                    j = i - 5
                    r = eng.tensor_tensor(u[:, j, :], SC[:, 0:P], u[:, j, :], ALU.add)
                r.then_inc(S["scan_ok"], 1)

            def hs_lo_(b, j):
                eng.wait_ge(S["hs_hi_ok"], body_at("hs_hi_ok", b, j))
                src = u[:, j, :] if j < L - 1 else carry[:, 1:P + 1]
                eng.tensor_tensor(hs_lo[:, j % 2, :], src, hs_hi[:, j % 2, :].bitcast(F32), ALU.subtract)\
                   .then_inc(S["hs_lo_ok"], 1)

            def attn(b, j):
                eng.wait_ge(S["y_done"], body_at("y_done", b, j))
                eng.wait_ge(S["gate_ok"], body_at("gate_ok", b, j))
                eng.tensor_tensor(work[:, j, :], tm_bank("y", j)[:, :], work[:, j, :], ALU.mult)\
                   .then_inc(S["v_ok"], 1)
                eng.wait_ge(S["v_ok"], body_at("v_ok", b, j))
                stats(work[:, j, :], 1, mvv[:, j, :])
                eng.tensor_scalar(rsv[:, j:j + 1], mvv[:, j, 1:2], EPS, None, ALU.add).then_inc(S["v_var"], 1)

            def attn_norm(b, j):
                eng.wait_ge(S["v_rs"], body_at("v_rs", b, j))
                eng.tensor_scalar(work[:, j, :], work[:, j, :], mvv[:, j, 0:1], rsv[:, j:j + 1],
                                  ALU.subtract, ALU.mult).then_inc(S["vn_ok"], 1)

            def x1_stats(b, j):
                eng.wait_ge(S["x1_ok"], body_at("x1_ok", b, j))
                stats(xres[:, j, :], 2, mvx[:, j, :])
                eng.tensor_scalar(rsx[:, j:j + 1], mvx[:, j, 1:2], EPS, None, ALU.add).then_inc(S["x1_var"], 1)

            def x1_norm(b, j):
                eng.wait_ge(S["x1_rs"], body_at("x1_rs", b, j))
                eng.tensor_scalar(work[:, j, :], xres[:, j, :], mvx[:, j, 0:1], rsx[:, j:j + 1],
                                  ALU.subtract, ALU.mult).then_inc(S["xn2_ok"], 1)

            def t_lo(mode, b, n, j):
                eng.wait_ge(S["t_hi"], body_at("t_hi", b, j))
                bank = TR[mode.tr_slot(f"t{j}")[0]]
                eng.tensor_tensor(x2T_lo[:, j % MS, :, :], bank[:, :].rearrange("p (k n) -> p k n", n=P),
                                  x2T_hi[:, j % MS, :, :].bitcast(F32), ALU.subtract).then_inc(S["t_lo"], 1)

            def ft_lo(mode, b, n, j):
                eng.wait_ge(S["ft_hi"], prep_at("ft_hi", n, j))
                bank = TR[mode.tr_slot(f"f{j}")[0]]
                eng.tensor_tensor(xT_lo[:, j, :, :], bank[:, :].rearrange("p (k n) -> p k n", n=P),
                                  xT_hi[:, j, :, :].bitcast(F32), ALU.subtract).then_inc(S["ft_lo"], 1)

            def h1(mode, b, n, m, f):
                name, i = f"h{m}{f}", KF * m + f
                h = hf[:, mode.hf_slot(name)[0], :]
                eng.wait_ge(S["sig_ok"], prep_at("sig_ok", n, i))
                eng.scalar_tensor_tensor(out=h, in0=FM[mode.fm_slot(name)[0]][:, :], scalar=b_col[:, f:f + 1], in1=h,
                                         op0=ALU.add, op1=ALU.mult).then_inc(S["h1_ok"], 1)
                eng.wait_ge(S["h1_ok"], prep_at("h1_ok", n, i))
                if m or mode is not PREPARE:
                    eng.wait_ge(S["s_done"], prep_at("s_done", n if m else n - 1, (m - 1) % NM))
                eng.tensor_copy(h1_hi[:, f, :], h).then_inc(S["h1hi_ok"], 1)

            def u_of(mode, b, n, m):
                eng.wait_ge(S["s_ok"], prep_at("s_ok", n, m))
                eng.wait_ge(S["b_done"], prep_at("b_done", n, m))
                if mode is not PREPARE:
                    eng.wait_ge(S["hs_hi_ok"], body_at("hs_hi_ok", b, L - 1))
                js = slice(m * MS, (m + 1) * MS)
                eng.scalar_tensor_tensor(out=u[:, js, :].rearrange("p a b -> p (a b)"),
                                         in0=FM[mode.fm_slot(f"b{m}")[0]][:, :], scalar=b_col[:, 3:4],
                                         in1=sg[:, :], op0=ALU.add, op1=ALU.mult).then_inc(S["u_ok"], 1)

            def h2hi(mode, b, n, m, f):
                i = KF * m + f
                eng.wait_ge(S["sq_ok"], body_at("sq_ok", b, i))
                if m:
                    eng.wait_ge(S["w2_done"], body_at("w2_done", b, m * MS - 1))
                else:
                    eng.wait_ge(S["w2_done"], body_at("w2_done", b - 1, L - 1))
                eng.tensor_copy(h2_hi[:, f, :], hf[:, mode.hf_slot(f"w{m}{f}")[0], :]).then_inc(S["h2hi_ok"], 1)

            def top(mode, b, n, m):
                eng.wait_ge(S["rt_done"], body_at("rt_done", b, m))
                link(eng.tensor_copy(lgt[:, :], SC[:, 0:MS * NE]))
                for s in range(MS):
                    r = eng.max(mx8[:, s, :], lgt[:, s * NE:(s + 1) * NE])
                r.then_inc(S["top_ok"], 1)
                eng.wait_ge(S["top_ok"], body_at("top_ok", b, m))
                link(eng.tensor_tensor(dif[:, bass.ds(b * L + m * MS, MS)] if not isinstance(b, int)
                                       else dif[:, b * L + m * MS:b * L + (m + 1) * MS],
                                       mx8[:, :, 1], mx8[:, :, 0], ALU.subtract))

            def z_stats(b, j):
                eng.wait_ge(S["w2_done"], body_at("w2_done", b, j))
                stats(tm_bank("z", j)[:, :], 3, mvz[:, j, :])
                eng.tensor_scalar(rsz[:, j:j + 1], mvz[:, j, 1:2], EPS, None, ALU.add).then_inc(S["z_var"], 1)

            def z_shift(b, j):
                eng.wait_ge(S["z_rs"], body_at("z_rs", b, j))
                eng.scalar_tensor_tensor(out=nmz[:, j:j + 1], in0=mvz[:, j, 0:1], scalar=-1.0, in1=rsz[:, j:j + 1],
                                         op0=ALU.mult, op1=ALU.mult).then_inc(S["z_nm"], 1)

            def batch(mode, b):
                n = b + 1
                prep = mode is LOOP
                a = (mode, b, n)
                for i in range(12):
                    scan_add(b, i)
                    if prep and i >= 4:
                        ln1_stats(n, i - 4)
                if prep:
                    for j in range(MS):
                        ln1_norm(n, j)
                hs_lo_(b, 0)
                hs_lo_(b, 1)
                attn(b, 0)
                hs_lo_(b, 2)
                if prep:
                    for j in range(MS, L):
                        ln1_norm(n, j)
                attn_norm(b, 0)
                for j in range(1, L + 1):
                    if j < L:
                        attn(b, j)
                        if j + 2 < L:
                            hs_lo_(b, j + 2)
                    x1_stats(b, j - 1)
                    if j < L:
                        attn_norm(b, j)
                    x1_norm(b, j - 1)
                    if 2 <= j <= 5:
                        t_lo(*a, j - 2)
                    if prep and j == 4:
                        ft_lo(*a, 0)
                    if prep and j == 5:
                        ft_lo(*a, 1)
                    if j == 6:
                        if prep:
                            ft_lo(*a, 2)
                        h2hi(*a, 0, 0)
                    if j == 7:
                        h2hi(*a, 0, 1)
                        if prep:
                            ft_lo(*a, 3)
                t_lo(*a, 4)
                top(*a, 0)
                if prep:
                    h1(*a, 0, 0)
                    h1(*a, 0, 1)
                t_lo(*a, 5)
                z_stats(b, 0)
                z_stats(b, 1)
                z_shift(b, 0)
                z_shift(b, 1)
                t_lo(*a, 6)
                z_stats(b, 2)
                z_stats(b, 3)
                z_shift(b, 2)
                z_shift(b, 3)
                if prep:
                    u_of(*a, 0)
                    ft_lo(*a, 4)
                t_lo(*a, 7)
                if prep:
                    ft_lo(*a, 5)
                    ft_lo(*a, 6)
                    ft_lo(*a, 7)
                h2hi(*a, 1, 0)
                h2hi(*a, 1, 1)
                if prep:
                    h1(*a, 1, 0)
                    h1(*a, 1, 1)
                top(*a, 1)
                for j in (4, 5, 6, 7):
                    z_stats(b, j)
                    if j > 4:
                        z_shift(b, j - 1)
                z_shift(b, 7)
                if prep:
                    u_of(*a, 1)

            eng.memset(carry[:, 0:1], 0.0)
            for t in (ones2, bias_y, bias_g):
                r = eng.memset(t[:, :].bitcast(F32), 0.0)
            r.then_inc(setup_dve, 1)
            copied = [0]

            def copy_power(dst):
                copied[0] += 1
                eng.wait_ge(pw_mm, copied[0])
                eng.tensor_copy(dst, SC[:, 0:P]).then_inc(pw_cp, 1)

            idx = {k: i for i, k in enumerate(POW)}
            k = 1
            while k < POW[-1]:
                if 2 * k < POW[-1]:
                    copy_power(PP[(k.bit_length() - 1) % 2])
                copy_power(apt[:, idx[2 * k], :])
                if k == 1:
                    copy_power(apt[:, idx[3], :])
                if k == 2:
                    for q in (5, 6, 7):
                        copy_power(apt[:, idx[q], :])
                if 3 * k in (24, 96, 384):
                    copy_power(apt[:, idx[3 * k], :])
                k *= 2
            for i, (name, hi, lo) in enumerate(SPLITS):
                eng.wait_ge(setup_act, i + 1)
                eng.tensor_tensor(lo, raw[name], hi.bitcast(F32), ALU.subtract).then_inc(setup_dve, 1)
            eng.wait_ge(setup_act, 9)
            eng.tensor_tensor(R_hi[:, :, NE:RC], kt(raw["r"], NE), R_hi[:, :, 0:NE].bitcast(F32), ALU.subtract)\
               .then_inc(setup_dve, 1)
            eng.wait_ge(setup_dve, 10)
            eng.wait_ge(w_ld[4], 16 * 8)
            for row, _, raw_row in BIAS_ROWS:
                r = slice(row, row + 1)
                dst = (bias_y if raw_row is brow else bias_g)[r, :]
                link(eng.tensor_copy(dst, raw_row[r, :]))
                if row % 64:
                    link(eng.tensor_tensor(dst, raw_row[r, :], dst.bitcast(F32), ALU.subtract))
            for row in (0, 32, 64, 96):
                link(eng.memset(ones2[row:row + 1, :].bitcast(F32), 1.0))
            eng.memset(flag[:, 0:1], 0.0).then_inc(setup_dve, 1)
            for j in range(L):
                ln1_stats(0, j)
            for j in range(L):
                ln1_norm(0, j)
            a = (PREPARE, 0, 0)
            for m in range(NM):
                for j in range(m * MS, (m + 1) * MS):
                    ft_lo(*a, j)
                for f in range(KF):
                    h1(*a, m, f)
                u_of(*a, m)
            with eng.Fori(0, NB - 1) as b:
                batch(LOOP, b)
            batch(LAST, NB - 1)
            eng.memset(flag[:, 1:2], 0.0).then_inc(chain_end, 1)
            eng.wait_ge(exp_ok, 1)
            eng.tensor_scalar(dif[:, :], dif[:, :], 1.0, None, ALU.add).then_inc(flag_dve, 1)
            eng.wait_ge(flag_dve, 1)
            eng.reciprocal(dif[:, :], dif[:, :]).then_inc(flag_dve, 1)
            eng.wait_ge(flag_dve, 2)
            eng.tensor_scalar(dif[:, :], dif[:, :], 1.0, None, ALU.is_ge).then_inc(flag_dve, 1)
            eng.wait_ge(flag_dve, 3)
            eng.tensor_reduce(flag[:, 0:1], dif[:, :], AX.X, ALU.max).then_inc(flag_dve, 1)
            eng.wait_ge(flag_pool, 1)
            eng.tensor_copy(flag_i[:, :], flag[:, 1:2]).then_inc(flag_ok, 1)

            def routed_norm(dst, src):
                link(eng.bn_stats(st6[:, 0, :], src))
                link(eng.bn_aggr(q_mv, st6[:, 0, :]))
                eng.tensor_scalar(q_rs, q_mv[:, 1:2], EPS, None, ALU.add).then_inc(EDGE["var"], 1)
                take(eng, "rs")
                return eng.tensor_scalar(dst, src, q_mv[:, 0:1], q_rs, ALU.subtract, ALU.mult)

            with if_routed(eng):
                with eng.Fori(0, NT) as t:
                    take(eng, "x_in", 16)
                    routed_norm(q_xn, q_x1).then_inc(EDGE["xn"], 1)
                    take(eng, "lg")
                    link(eng.tensor_copy(q_lg, SC[:, 0:NE]))
                    link(eng.max(q_mx, q_lg))
                    eng.tensor_tensor(q_d, q_mx[:, 1:2], q_mx[:, 0:1], ALU.subtract).then_inc(EDGE["d"], 1)
                    take(eng, "e")
                    link(eng.tensor_scalar(q_d, q_d, 1.0, None, ALU.add))
                    link(eng.reciprocal(q_d, q_d))
                    link(eng.tensor_scalar(q_d, q_d, 1.0, None, ALU.is_ge))
                    link(eng.tensor_scalar(q_pr, q_lg, q_mx[:, 0:1], q_d, ALU.is_equal, ALU.mult))
                    eng.memset(flag[:, 2:3], 0.0).then_inc(EDGE["pr"], 1)
                    take(eng, "y")
                    link(eng.tensor_copy(q_acc, TM[1][:, :]))
                    eng.sem_inc(EDGE["acc"], 1)
                    with eng.Fori(0, NE) as e:
                        take(eng, "y")
                        link(eng.scalar_tensor_tensor(out=q_acc, in0=TM[1][:, :], scalar=q_pr[:, bass.ds(e, 1)],
                                                      in1=q_acc, op0=ALU.mult, op1=ALU.add))
                        eng.sem_inc(EDGE["acc"], 1)
                    link(routed_norm(q_xn, q_acc))
                    eng.tensor_tensor(q_o, q_xn, q_x1, ALU.add).then_inc(EDGE["o_ok"], 1)

        @block.gpsimd
        def _(eng):
            eng.memset(negh[:, :], -0.5).then_inc(pchain, 1)
            eng.wait_ge(pchain, 1)
            credits(eng, ["v_rs", "x1_ok", "x1_rs", "h2lo_ok", "z_rs", "out_ok"])

            def power(dst, src, n):
                return eng.tensor_tensor(dst, src, negh[:, 0:n], ALU.pow)

            def ln1_rs(n, m):
                eng.wait_ge(S["l1_var"], prep_at("l1_var", n, m))
                js = slice(m * MS, (m + 1) * MS)
                power(rs1[:, js], ve1[:, js], MS).then_inc(S["l1_rs"], 1)

            def v_rs(b, j):
                eng.wait_ge(S["v_var"], body_at("v_var", b, j))
                power(rsv[:, j:j + 1], rsv[:, j:j + 1], 1).then_inc(S["v_rs"], 1)

            def x1_rs(b, j):
                eng.wait_ge(S["x1_var"], body_at("x1_var", b, j))
                power(rsx[:, j:j + 1], rsx[:, j:j + 1], 1).then_inc(S["x1_rs"], 1)

            def z_rs(b, j):
                eng.wait_ge(S["z_var"], body_at("z_var", b, j))
                power(rsz[:, j:j + 1], rsz[:, j:j + 1], 1).then_inc(S["z_rs"], 1)

            def x1(b, j):
                if j == 0:
                    eng.wait_ge(S["xres_ld"], body_at("xres_ld", b))
                eng.wait_ge(S["vn_ok"], body_at("vn_ok", b, j))
                eng.tensor_tensor(xres[:, j, :], work[:, j, :], xres[:, j, :], ALU.add).then_inc(S["x1_ok"], 1)

            def outs(b, j):
                eng.wait_ge(S["zn_ok"], body_at("zn_ok", b, j))
                eng.tensor_tensor(work[:, j, :], work[:, j, :], xres[:, j, :], ALU.add).then_inc(S["out_ok"], 1)

            def h1_lo_(mode, b, n, m, f):
                name, i = f"h{m}{f}", KF * m + f
                eng.wait_ge(S["h1hi_ok"], prep_at("h1hi_ok", n, i))
                eng.tensor_tensor(h1_lo[:, f, :], hf[:, mode.hf_slot(name)[0], :], h1_hi[:, f, :].bitcast(F32),
                                  ALU.subtract).then_inc(S["h1lo_ok"], 1)

            def h2_lo_(mode, b, n, m, f):
                name, i = f"w{m}{f}", KF * m + f
                eng.wait_ge(S["h2hi_ok"], body_at("h2hi_ok", b, i))
                eng.tensor_tensor(h2_lo[:, f, :], hf[:, mode.hf_slot(name)[0], :], h2_hi[:, f, :].bitcast(F32),
                                  ALU.subtract).then_inc(S["h2lo_ok"], 1)

            def batch(mode, b):
                n = b + 1
                prep = mode is LOOP
                a = (mode, b, n)
                if prep:
                    ln1_rs(n, 0)
                    ln1_rs(n, 1)
                v_rs(b, 0)
                x1(b, 0)
                for j in range(1, L + 1):
                    if j < L:
                        v_rs(b, j)
                    x1_rs(b, j - 1)
                    if j < L:
                        x1(b, j)
                    if j in (6, 7):
                        h2_lo_(*a, 0, j - 6)
                if prep:
                    h1_lo_(*a, 0, 0)
                    h1_lo_(*a, 0, 1)
                for j in (0, 2):
                    z_rs(b, j)
                    z_rs(b, j + 1)
                    outs(b, j)
                    outs(b, j + 1)
                h2_lo_(*a, 1, 0)
                h2_lo_(*a, 1, 1)
                if prep:
                    h1_lo_(*a, 1, 0)
                    h1_lo_(*a, 1, 1)
                z_rs(b, 4)
                for j in (4, 5, 6, 7):
                    if j < 7:
                        z_rs(b, j + 1)
                    outs(b, j)

            a = (PREPARE, 0, 0)
            for m in range(NM):
                ln1_rs(0, m)
            for m in range(NM):
                for f in range(KF):
                    h1_lo_(*a, m, f)
            with eng.Fori(0, NB - 1) as b:
                batch(LOOP, b)
            batch(LAST, NB - 1)
            eng.wait_ge(flag_dve, 4)
            eng.partition_all_reduce(flag[:, 1:2], flag[:, 0:1], P, bass.bass_isa.ReduceOp.max).then_inc(flag_pool, 1)

            with if_routed(eng):
                with eng.Fori(0, 2 * NT) as t:
                    take(eng, "var")
                    power(q_rs, q_rs, 1).then_inc(EDGE["rs"], 1)


def kernel(**inputs):
    import numpy as np
    import concourse.bacc as bacc
    from concourse.bass_utils import run_bass_kernel_spmd

    nc = bacc.Bacc("TRN2", target_bir_lowering=False, num_devices=1)
    a = {k.replace("L0_attn_", "").replace("L0_ffn_", ""): np.asarray(v) for k, v in inputs.items()}
    names = ["x", "A", ("A", 1), ("B_w", 1), "B_b", ("C_w", 1), "C_b", ("D_w", 1), "D_b", ("s_w1", 1), "s_b1",
             ("s_w2", 1), "s_b2", ("g_w", 1), "g_b", "Ws1", "Ws2", "W1", "W2", "Wr"]
    arrays, args = {}, []

    def give(name, array):
        array = np.ascontiguousarray(array)
        arrays[name] = array
        args.append(nc.dram_tensor(name, array.shape, mybir.dt.from_np(array.dtype), kind="ExternalInput").ap())

    for n in names:
        if isinstance(n, tuple):
            give(f"in_{n[0]}_t", a[n[0]].T)
        else:
            give(f"in_{n}", a[n])
    give("in_eye", np.eye(P, dtype=np.float32))
    out = nc.dram_tensor("out_0", a["x"].shape, F32, kind="ExternalOutput").ap()
    build(nc, *args, out)
    r = run_bass_kernel_spmd(nc, [arrays], core_ids=[0])
    return r.results[0]["out_0"]
```

```python
from contextlib import ExitStack

import concourse.bass as bass
from concourse import mybir

ALU = mybir.AluOpType
ACT = mybir.ActivationFunctionType
AX = mybir.AxisListType
F32 = mybir.dt.float32
F32R = mybir.dt.float32r
I32 = mybir.dt.int32

P = 128
EPS = 1e-5


def build(nc, x, A, AT, BwT, Bb, CwT, Cb, DwT, Db, s1T, s1b, s2T, s2b, gwT, gb, Ws1, Ws2, W1, W2, Wr, eye, out):
    NB, T, D = x.shape
    NS = A.shape[0]
    NE, _, FH = W1.shape
    KD = D // P
    KF = FH // P
    L = T // P
    MS = 4
    NM = L // MS
    assert NS == P and D == 512 and FH == 256 and L == 8 and T == P * L

    x_v = x.rearrange("b (c j) d -> b c j d", j=L)
    out_v = out.rearrange("b (c j) d -> b c j d", j=L)
    x1_dram = nc.dram_tensor("x1_scratch", [NB, T, D], F32).ap()
    x1_v = x1_dram.rearrange("b (c j) d -> b c j d", j=L)

    with ExitStack() as ctx:
        def sb(name, shape, dt=F32):
            return ctx.enter_context(nc.sbuf_tensor(name, shape, dt))

        def sem(name):
            return ctx.enter_context(nc.semaphore(name))

        def pair(name, cols):
            return sb(name + "_hi", [P, cols], F32R), sb(name + "_lo", [P, cols], F32R)

        s1_w = pair("s1w", KD * FH)
        s2_w = pair("s2w", KF * NS)
        b_w = pair("bw", KD * NS)
        c_w = pair("cw", D)
        d_w = pair("dw", KD * D)
        g_w = pair("gw", KD * D)
        f1_w = pair("f1w", KD * FH)
        RC = 2 * NE
        f2_hi = sb("f2w_hi", [P, KD * RC + KF * D], F32R)
        f2_lo = sb("f2w_lo", [P, KF * D], F32R)
        ones2 = sb("ones2", [P, P], F32R)
        bias_y = sb("bias_y", [P, D], F32R)
        bias_g = sb("bias_g", [P, D], F32R)

        xin = sb("xin", [P, L, D])
        xres = sb("xres", [P, L, D])
        work = sb("work", [P, L, D])
        xT_hi = sb("xT_hi", [P, L, KD, P], F32R)
        xT_lo = sb("xT_lo", [P, L, KD, P], F32R)
        x2T_hi = sb("x2T_hi", [P, MS, KD, P], F32R)
        x2T_lo = sb("x2T_lo", [P, MS, KD, P], F32R)
        h1_hi = sb("h1_hi", [P, KF, MS * P], F32R)
        h1_lo = sb("h1_lo", [P, KF, MS * P], F32R)
        h2_hi = sb("h2_hi", [P, KF, MS * P], F32R)
        h2_lo = sb("h2_lo", [P, KF, MS * P], F32R)
        hf = sb("hf", [P, 2, MS * P])
        sg = sb("sg", [P, MS * P])
        u = sb("u", [P, L, P])
        carry = sb("carry", [P, P + 1])
        hs_hi = sb("hs_hi", [P, 2, P], F32R)
        hs_lo = sb("hs_lo", [P, 2, P], F32R)
        POW = [1, 2, 3, 4, 5, 6, 7, 8, 16, 24, 32, 64, 96, 128, 256, 384, 512]
        apt = sb("apt", [P, len(POW), P])
        ident = sb("ident", [P, P])
        comb = sb("comb", [RC, NE])
        b_col = sb("b_col", [P, 4])
        negh = sb("negh", [P, MS])
        first_sigmoid = sb("first_sigmoid", [P, 1])
        st6 = sb("st6", [P, 4, 6])
        mv1 = sb("mv1", [P, L, 2])
        ve1 = sb("ve1", [P, L])
        rs1 = sb("rs1", [P, L])
        mvv = sb("mvv", [P, L, 2])
        rsv = sb("rsv", [P, L])
        mvx = sb("mvx", [P, L, 2])
        rsx = sb("rsx", [P, L])
        mvz = sb("mvz", [P, L, 2])
        rsz = sb("rsz", [P, L])
        nmz = sb("nmz", [P, L])
        lgt = sb("lgt", [P, MS * NE])
        mx8 = sb("mx8", [P, MS, 8])
        dif = sb("dif", [P, NB * L])
        flag = sb("flag", [P, 4])
        flag_i = sb("flag_i", [P, 1], I32)

        TR = [ctx.enter_context(nc.psum_tensor(f"TR{i}", [P, 512], F32)) for i in range(2)]
        TM = [ctx.enter_context(nc.psum_tensor(f"TM{i}", [P, 512], F32)) for i in range(3)]
        FM = [ctx.enter_context(nc.psum_tensor(f"FM{i}", [P, 512], F32)) for i in range(2)]
        SC = ctx.enter_context(nc.psum_tensor("SC", [P, 512], F32))

        BODY = dict(g_done=L, scan_done=12, y_done=L, t_done=L, w1_done=NM * KF, r_done=NM, rt_done=NM, w2_done=L,
                    gate_ok=L, hs_hi_ok=L, t_hi=L, relu_ok=NM * KF, sq_ok=NM * KF, lg_ok=NM, zn_ok=L,
                    scan_ok=12, hs_lo_ok=L, v_ok=L, v_var=L, vn_ok=L, x1_var=L, xn2_ok=L, t_lo=L, h2hi_ok=NM * KF,
                    z_var=L, z_nm=L, top_ok=NM,
                    v_rs=L, x1_ok=L, x1_rs=L, h2lo_ok=NM * KF, z_rs=L, out_ok=L,
                    xres_ld0=16, xres_ld1=16, x1_st0=16, x1_st1=16, out_st0=16, out_st1=16)
        PREP = dict(ft_done=L, h_done=NM * KF, b_done=NM, s_done=NM,
                    ft_hi=L, sig_ok=NM * KF, s_ok=NM,
                    l1_var=NM, xn_ok=L, ft_lo=L, h1_ok=NM * KF, h1hi_ok=NM * KF, u_ok=NM,
                    l1_rs=NM, h1lo_ok=NM * KF, xin_ld0=16, xin_ld1=16)
        S = {n: sem(n) for n in (*BODY, *PREP)}
        w_ld = {n: sem("ld_" + n)
                for n in ("a", "comb", "small", "s1", "b", "s2", "bias", "g", "d", "c", "f1", "f2", "r")}
        chain = sem("dve_chain")
        hi_ok = sem("weights_hi")
        lo_dve = sem("weights_lo_dve")
        lo_pool = sem("weights_lo_pool")
        pw_mm = sem("power_multiplied")
        pw_cp = sem("power_copied")
        last_out = sem("last_outs")
        last_st = sem("last_stores")
        diffs_ok = sem("logits_done")
        exp_ok = sem("exp_ok")
        flag_dve = sem("flag_dve")
        flag_pool = sem("flag_pool")
        flag_ok = sem("flag_ok")
        EDGE = {n: sem("routed_" + n) for n in (
            "x_in", "o_ok", "o_st", "w_in0", "w_in1", "w_free", "ws_in", "var", "rs", "xn", "tr", "xt", "lg", "d", "e",
            "pr", "h", "hr", "hr1", "y", "acc")}

        def body_at(name, b, i=0):
            k = BODY[name]
            return b * k + (k if k == 16 else i + 1)

        def prep_at(name, n, i=0):
            k = PREP[name]
            return n * k + (k if k == 16 else i + 1)

        xres_f = xres[:, :, :].rearrange("p a b -> p (a b)")
        work_f = work[:, :, :].rearrange("p a b -> p (a b)")
        brow, grow = u[:, 0:MS, :].rearrange("p a b -> p (a b)"), sg[:, :]
        PA = u[:, L - 2, :]
        PP = [u[:, L - 1, :], carry[:, 1:P + 1]]
        raw = {"s1": work_f[:, 0:KD * FH], "b": work_f[:, KD * FH:KD * (FH + NS)],
               "s2": u[:, MS:MS + KF, :].rearrange("p a b -> p (a b)"),
               "by": brow, "bg": grow,
               "g": xres_f[:, KD * D:2 * KD * D], "d": xres_f[:, 0:KD * D], "c": work_f[:, 3 * D:4 * D],
               "f1": work_f[:, 4 * D:4 * D + KD * FH], "f2": work_f[:, 6 * D:6 * D + KF * D],
               "r": lgt[:, :]}
        BIAS_ROWS = [(0, Cb, brow), (32, Cb, brow), (64, Db, brow), (96, Db, brow), (0, gb, grow), (32, gb, grow)]

        def kt(ap, n):
            return ap.rearrange("p (k n) -> p k n", n=n)

        R_hi = f2_hi[:, 0:KD * RC].rearrange("p (k c) -> p k c", c=RC)
        F2H = f2_hi[:, KD * RC:]

        PARTS = {"s1": s1_w, "b": b_w, "s2": s2_w, "by": (bias_y, bias_y), "bg": (bias_g, bias_g), "g": g_w, "d": d_w,
                 "c": c_w, "f1": f1_w}
        PARTS = {n: (hi[:, :], lo[:, :]) for n, (hi, lo) in PARTS.items()}
        PARTS["f2"] = (F2H, f2_lo[:, :])
        PARTS["r"] = (R_hi[:, :, 0:NE], R_hi[:, :, NE:RC])
        raw["r"] = kt(raw["r"], NE)
        HI = {n: i + 1 for i, n in enumerate(PARTS)}
        LO_DVE = {n: i + 1 for i, n in enumerate(["constants", "b", "s2", "biases"])}
        LO_POOL = {n: i + 1 for i, n in enumerate(["constants", "s1", "g", "d", "c", "f1", "f2", "r"])}

        def low_part(eng, name):
            eng.wait_ge(hi_ok, HI[name])
            return eng.tensor_tensor(PARTS[name][1], raw[name], PARTS[name][0].bitcast(F32), ALU.subtract)

        at = {k: apt[:, i, :] for i, k in enumerate(POW)}
        POWERS = []
        k, plain = 1, PA
        while k < POW[-1]:
            twice = PP[(k.bit_length() - 1) % 2]
            if 2 * k < POW[-1]:
                POWERS.append((twice, at[k], plain))
            POWERS.append((at[2 * k], plain, at[k]))
            POWERS += [(at[q], PA, at[q - 1]) for q in {1: (3,), 2: (5, 6, 7)}.get(k, ())]
            if 3 * k in POW and k >= L:
                POWERS.append((at[3 * k], plain, at[2 * k]))
            k, plain = 2 * k, twice

        FIRST_BANKS = [*TM, *TR]

        LAST_BANKS = dict(zip(range(MS, L), (TM[2], TM[0], *TR)))

        def z_bank(rep, j):
            return LAST_BANKS[j] if rep == NB else tm_bank(f"z{j}")

        def ft_bank(rep, j):
            return FIRST_BANKS[j % len(FIRST_BANKS)] if rep < 0 else tr_bank(f"f{j}")

        TM_RING = (3, ["g0", "g1", "z4", "z5", "g2", "z6", "z7", "g3", "y0", "g4", "y1", "g5", "y2", "g6", "y3", "g7",
                       "y4", "y5", "y6", "y7", "z0", "z1", "z2", "z3"])
        FM_RING = (2, ["w10", "w11", "r1", "h00", "h01", "b0", "s0", "w00", "w01", "r0", "h10", "h11", "b1", "s1"])
        TR_RING = (2, ["f0", "t0", "f1", "t1", "f2", "f3", "t2", "t3", "f4", "f5", "f6", "f7", "t4", "t5", "t6", "t7"])
        HF_RING = (2, ["w10", "w11", "r1", "h00", "h01", "w00", "w01", "r0", "h10", "h11"])
        for size, order in (TM_RING, FM_RING, TR_RING, HF_RING):
            assert len(order) % size == 0
        TAIL = {"w10", "w11", "r1", "z4", "z5", "z6", "z7"}
        PREPS = {"f", "h", "b", "s"}

        def shift(name):
            return -1 if name in TAIL else 1 if name[0] in PREPS else 0

        def slot(ring, name):
            size, order = ring
            return order.index(name) % size

        def before(ring, name, rep):
            size, order = ring
            i, back = order.index(name), 0
            while True:
                i -= size
                if i < 0:
                    i, back = i + len(order), back - 1
                    if rep + back < -1:
                        return None, 0
                if 0 <= rep + back + shift(order[i]) < NB:
                    return order[i], back

        def tm_bank(name):
            return TM[slot(TM_RING, name)]

        def fm_bank(name):
            return FM[slot(FM_RING, name)]

        def tr_bank(name):
            return TR[slot(TR_RING, name)]

        def hf_row(name):
            return hf[:, slot(HF_RING, name), :]

        def wait_free(eng, ring, name, b, rep, freed):
            prev, back = before(ring, name, rep)
            if prev is None:
                return
            batch_of = b + (back + shift(prev))
            item = int(prev[1]) if len(prev) == 2 else KF * int(prev[1]) + int(prev[2])
            sem_name = freed[prev[0]]
            at = prep_at if sem_name in PREP else body_at
            eng.wait_ge(S[sem_name], at(sem_name, batch_of, item))

        TM_FREED = {"g": "gate_ok", "y": "v_ok", "z": "zn_ok"}
        FM_FREED = {"w": "relu_ok", "r": "top_ok", "h": "h1_ok", "b": "u_ok", "s": "s_ok"}
        TR_FREED = {"t": "t_lo", "f": "ft_lo"}
        HF_FREED = {"w": "h2lo_ok", "r": "rt_done", "h": "h1lo_ok"}

        NT = NB * L
        q_x1, q_xn, q_acc, q_o = (work[:, i, :] for i in range(4))
        q_xT = work[:, 4, :].rearrange("p (k n) -> p k n", n=P)
        q_h = [work[:, 5, i * FH:(i + 1) * FH].rearrange("p (f n) -> p f n", n=P) for i in range(2)]
        q_small = work[:, 6, :]
        q_mv, q_rs, q_d = q_small[:, 0:2], q_small[:, 2:3], q_small[:, 3:4]
        q_lg, q_mx, q_pr = q_small[:, 8:16], q_small[:, 16:24], q_small[:, 24:24 + NE]
        q_wr = xres[:, 0, 0:KD * NE].rearrange("p (k n) -> p k n", n=NE)

        def rows(t, i):
            return t[:, i:i + 2, :].rearrange("p a b -> p (a b)")

        q_w1 = [rows(xin, 0).rearrange("p (k n) -> p k n", n=FH), rows(xin, 4).rearrange("p (k n) -> p k n", n=FH)]
        q_w2 = [rows(xin, 2).rearrange("p (k n) -> p k n", n=D), rows(xin, 6).rearrange("p (k n) -> p k n", n=D)]
        q_s1 = rows(xres, 2).rearrange("p (k n) -> p k n", n=FH)
        q_s2 = rows(xres, 4).rearrange("p (k n) -> p k n", n=D)
        x1_t = x1_dram.rearrange("b t d -> (b t) d")
        out_t = out.rearrange("b t d -> (b t) d")

        def take(eng, name, n=1):
            eng.wait_ge(EDGE[name], n)
            eng.sem_inc(EDGE[name], -n)

        def if_routed(eng):
            eng.wait_ge(flag_ok, 1)
            return eng.If(eng.value_load(flag_i[0:1, 0:1], min_val=0, max_val=1) > 0)

        block = ctx.enter_context(nc.Block())

        @block.sync
        def _(eng):
            def load(name, src, n):
                eng.dma_start(raw[name] if name in ("c", "r") else kt(raw[name], n), src).then_inc(w_ld[name], 16)

            def tiles(w):
                return w.rearrange("(k p) n -> p k n", p=P)

            def load_x(b, m):
                js = slice(m * MS, (m + 1) * MS)
                eng.dma_start(xin[:, js, :], x_v[b][:, js, :]).then_inc(S[f"xin_ld{m}"], 16)

            load_x(0, 0)
            eng.dma_start(PA, A).then_inc(w_ld["a"], 16)
            eng.dma_start(at[1], AT).then_inc(w_ld["a"], 16)
            eng.dma_start(ident[:, :], eye).then_inc(w_ld["a"], 16)
            load("s1", tiles(s1T), FH)
            eng.wait_ge(lo_pool, LO_POOL["constants"])
            for row, src, dst in BIAS_ROWS:
                eng.dma_start(dst[row:row + 1, :], src[None, :]).then_inc(w_ld["bias"], 16)
            load_x(0, 1)
            load("b", tiles(BwT), NS)
            load("s2", tiles(s2T), NS)
            with nc.allow_non_contiguous_dma(reason="bias columns"):
                eng.dma_start(b_col[:, 0:2], s1b.rearrange("(k p) -> p k", p=P)).then_inc(w_ld["small"], 16)
                eng.dma_start(b_col[:, 2:3], s2b.rearrange("(k p) -> p k", p=P)).then_inc(w_ld["small"], 16)
                eng.dma_start(b_col[:, 3:4], Bb.rearrange("(k p) -> p k", p=P)).then_inc(w_ld["small"], 16)
            load("g", tiles(gwT), D)
            load("d", tiles(DwT), D)
            load("c", CwT, D)
            load("f1", tiles(Ws1), FH)
            load("f2", tiles(Ws2), D)
            load("r", tiles(Wr), NE)
            for row in (0, NE):
                eng.dma_start(comb[row:row + NE, :], eye[0:NE, 0:NE]).then_inc(w_ld["comb"], 16)

            def one_pass(b, rep):
                if rep + 1 < NB:
                    eng.wait_ge(S["ft_done"], prep_at("ft_done", b, L - 1))
                    for m in range(NM):
                        load_x(b + 1, m)
                if rep == 0:
                    eng.wait_ge(lo_pool, LO_POOL["d"])
                for m in range(NM):
                    js = slice(m * MS, (m + 1) * MS)
                    if rep > 0:
                        if m == NM - 1:
                            eng.wait_ge(S["out_ok"], body_at("out_ok", b - 1, L - 1))
                            eng.dma_start(out_v[b - 1][:, js, :], work[:, js, :]).then_inc(S[f"out_st{m}"], 16)
                        eng.wait_ge(S["x1_st" + str(m)], body_at("x1_st" + str(m), b - 1))
                        if m < NM - 1:
                            eng.wait_ge(S["out_ok"], body_at("out_ok", b - 1, m * MS + MS - 1))
                    eng.dma_start(xres[:, js, :], x_v[b][:, js, :]).then_inc(S[f"xres_ld{m}"], 16)
                for m in range(NM):
                    js = slice(m * MS, (m + 1) * MS)
                    eng.wait_ge(S["x1_ok"], body_at("x1_ok", b, m * MS + MS - 1))
                    eng.dma_start(x1_v[b][:, js, :], xres[:, js, :]).then_inc(S[f"x1_st{m}"], 16)
                for m in range(NM - 1):
                    js = slice(m * MS, (m + 1) * MS)
                    eng.wait_ge(S["out_ok"], body_at("out_ok", b, m * MS + MS - 1))
                    eng.dma_start(out_v[b][:, js, :], work[:, js, :]).then_inc(S[f"out_st{m}"], 16)

            one_pass(0, 0)
            with eng.Fori(1, NB - 1) as b:
                one_pass(b, 1)
            one_pass(NB - 1, NB - 1)
            for j in range(MS, L):
                if j < L - 2:
                    eng.wait_ge(S["out_ok"], body_at("out_ok", NB - 1, j))
                else:
                    eng.wait_ge(last_out, j - (L - 2) + 1)
                eng.dma_start(out_v[NB - 1][:, j, :], work[:, j, :]).then_inc(last_st, 16)
            eng.wait_ge(last_st, MS * 16)
            eng.wait_ge(S["out_st1"], body_at("out_st1", NB - 2))
            eng.wait_ge(S["out_st0"], body_at("out_st0", NB - 1))
            for m in range(NM):
                eng.wait_ge(S[f"x1_st{m}"], body_at(f"x1_st{m}", NB - 1))

            with if_routed(eng):
                eng.dma_start(q_s1, Ws1.rearrange("(k p) n -> p k n", p=P)).then_inc(EDGE["ws_in"], 16)
                eng.dma_start(q_s2, Ws2.rearrange("(k p) n -> p k n", p=P)).then_inc(EDGE["ws_in"], 16)
                eng.dma_start(q_wr, Wr.rearrange("(k p) n -> p k n", p=P)).then_inc(EDGE["ws_in"], 16)
                eng.sem_inc(EDGE["w_free"], 2)
                with eng.Fori(0, NT) as t:
                    eng.dma_start(q_x1, x1_t[bass.ts(t, P), :]).then_inc(EDGE["x_in"], 16)
                    with eng.Fori(0, NE // 2) as e:
                        for s in range(2):
                            take(eng, "w_free")
                            eng.dma_start(q_w1[s], W1[e * 2 + s].rearrange("(k p) n -> p k n", p=P))\
                               .then_inc(EDGE[f"w_in{s}"], 16)
                            eng.dma_start(q_w2[s], W2[e * 2 + s].rearrange("(k p) n -> p k n", p=P))\
                               .then_inc(EDGE[f"w_in{s}"], 16)
                    take(eng, "o_ok")
                    eng.dma_start(out_t[bass.ts(t, P), :], q_o).then_inc(EDGE["o_st"], 16)
                    take(eng, "o_st", 16)

        @block.tensor
        def _(eng):

            def mm3(ps, lhs, rhs, first, last):
                eng.matmul(ps, lhs[0], rhs[0], start=first, stop=False)
                eng.matmul(ps, lhs[0], rhs[1], start=False, stop=False)
                return eng.matmul(ps, lhs[1], rhs[0], start=False, stop=last)

            def power(i):
                if i == 0:
                    eng.wait_ge(w_ld["a"], 3 * 16)
                else:
                    eng.wait_ge(pw_cp, i)
                _, lhsT, rhs = POWERS[i]
                eng.matmul(SC[:, 0:P], lhsT, rhs, start=True, stop=True).then_inc(pw_mm, 1)

            def scan_step(b, rep, i):
                if i == 0:
                    eng.wait_ge(S["u_ok"], prep_at("u_ok", b, NM - 1))
                else:
                    eng.wait_ge(S["scan_ok"], body_at("scan_ok", b, i - 1))
                if i == 0:
                    for j in range(L - 1):
                        m = eng.matmul(SC[:, 0:P], at[L - 1 - j], u[:, j, :],
                                       start=(j == 0), stop=(j == L - 2))
                elif i <= 4:
                    s = 4 ** (i - 1)
                    reps = [r for r in (1, 2, 3) if r * s < P]
                    for r in reps:
                        m = eng.matmul(SC[:, r * s:P], at[L * s * r], carry[:, 1:1 + P - r * s],
                                       start=(r == 1), stop=(r == reps[-1]))
                else:
                    j = i - 5
                    prev = carry[:, 0:P] if j == 0 else u[:, j - 1, :]
                    m = eng.matmul(SC[:, 0:P], at[1], prev, start=True, stop=True)
                m.then_inc(S["scan_done"], 1)

            def G(b, rep, j, steps={}):
                wait_free(eng, TM_RING, f"g{j}", b, rep, TM_FREED)
                ps = tm_bank(f"g{j}")[:, :]
                eng.matmul(ps, ones2[:, :], bias_g[:, :], start=True, stop=False)
                for k in range(KD):
                    m = mm3(ps, (xT_hi[:, j, k, :], xT_lo[:, j, k, :]),
                            [w[:, k * D:(k + 1) * D] for w in g_w], False, k == KD - 1)
                    if k == KD - 1:
                        m.then_inc(S["g_done"], 1)
                    if k in steps:
                        scan_step(b, rep, steps[k])

            def Y(b, rep, j):
                wait_free(eng, TM_RING, f"y{j}", b, rep, TM_FREED)
                ps = tm_bank(f"y{j}")[:, :]
                eng.matmul(ps, ones2[:, :], bias_y[:, :], start=True, stop=False)
                for k in range(KD):
                    mm3(ps, (xT_hi[:, j, k, :], xT_lo[:, j, k, :]),
                        [w[:, k * D:(k + 1) * D] for w in d_w], False, False)
                eng.wait_ge(S["hs_hi_ok"], body_at("hs_hi_ok", b, j))
                eng.wait_ge(S["hs_lo_ok"], body_at("hs_lo_ok", b, j))
                mm3(ps, (hs_hi[:, j % 2, :], hs_lo[:, j % 2, :]), [w[:, :] for w in c_w], False, True)\
                    .then_inc(S["y_done"], 1)

            def transposes(bank, src):
                for k in range(KD):
                    m = eng.transpose(bank[:, k * P:(k + 1) * P], src[:, k * P:(k + 1) * P], ident[:, :])
                return m

            def T(b, rep, j):
                wait_free(eng, TR_RING, f"t{j}", b, rep, TR_FREED)
                eng.wait_ge(S["xn2_ok"], body_at("xn2_ok", b, j))
                transposes(tr_bank(f"t{j}"), work[:, j, :]).then_inc(S["t_done"], 1)

            def FT(b, rep, j):
                if rep >= 0:
                    wait_free(eng, TR_RING, f"f{j}", b, rep, TR_FREED)
                elif j >= len(FIRST_BANKS):
                    eng.wait_ge(S["ft_lo"], prep_at("ft_lo", 0, j - len(FIRST_BANKS)))
                eng.wait_ge(S["xn_ok"], prep_at("xn_ok", b + 1, j))
                transposes(ft_bank(rep, j), xin[:, j, :]).then_inc(S["ft_done"], 1)

            def W1f(b, rep, m, f):
                name = f"w{m}{f}"
                i = b + shift(name)
                if f == 0:
                    eng.wait_ge(S["t_hi"], body_at("t_hi", i, m * MS + MS - 1))
                    eng.wait_ge(S["t_lo"], body_at("t_lo", i, m * MS + MS - 1))
                wait_free(eng, FM_RING, name, b, rep, FM_FREED)
                for k in range(KD):
                    o = k * FH + f * P
                    r = mm3(fm_bank(name)[:, :], [w[:, o:o + P] for w in f1_w],
                            (x2T_hi[:, :, k, :], x2T_lo[:, :, k, :]), k == 0, k == KD - 1)
                r.then_inc(S["w1_done"], 1)

            def R(b, rep, m):
                wait_free(eng, FM_RING, f"r{m}", b, rep, FM_FREED)
                for k in range(KD):
                    w = f2_hi[:, k * RC:k * RC + P]
                    eng.matmul(fm_bank(f"r{m}")[:, :], w, x2T_hi[:, :, k, :], start=(k == 0), stop=False)
                    r = eng.matmul(fm_bank(f"r{m}")[:, :], w, x2T_lo[:, :, k, :], start=False, stop=(k == KD - 1))
                r.then_inc(S["r_done"], 1)

            def RT(b, rep, m):
                i = b + shift(f"r{m}")
                eng.wait_ge(S["lg_ok"], body_at("lg_ok", i, m))
                lg = hf_row(f"r{m}")[0:RC, :]
                for s in range(MS):
                    r = eng.matmul(fm_bank(f"r{m}")[:, s * NE:(s + 1) * NE], lg[:, s * P:(s + 1) * P], comb[:, :],
                                   start=True, stop=True)
                r.then_inc(S["rt_done"], 1)

            def W2(b, rep, j):
                m, s = divmod(j, MS)
                i = b + shift(f"z{j}")
                if s == 0:
                    eng.wait_ge(S["h2hi_ok"], body_at("h2hi_ok", i, KF * m + KF - 1))
                    eng.wait_ge(S["h2lo_ok"], body_at("h2lo_ok", i, KF * m + KF - 1))
                if rep < NB or j < MS + 2:
                    wait_free(eng, TM_RING, f"z{j}", b, rep, TM_FREED)
                else:
                    eng.wait_ge(S["t_lo"], body_at("t_lo", i, L - 1))
                for f in range(KF):
                    c = slice(s * P, (s + 1) * P)
                    r = mm3(z_bank(rep, j)[:, :], (h2_hi[:, f, c], h2_lo[:, f, c]),
                            (F2H[:, f * D:(f + 1) * D], f2_lo[:, f * D:(f + 1) * D]), f == 0, f == KF - 1)
                r.then_inc(S["w2_done"], 1)

            def H(b, rep, m, f):
                name = f"h{m}{f}"
                if f == 0:
                    eng.wait_ge(S["ft_hi"], prep_at("ft_hi", b + 1, m * MS + MS - 1))
                    eng.wait_ge(S["ft_lo"], prep_at("ft_lo", b + 1, m * MS + MS - 1))
                wait_free(eng, FM_RING, name, b, rep, FM_FREED)
                js = slice(m * MS, (m + 1) * MS)
                for k in range(KD):
                    o = k * FH + f * P
                    r = mm3(fm_bank(name)[:, :], [w[:, o:o + P] for w in s1_w],
                            (xT_hi[:, js, k, :], xT_lo[:, js, k, :]), k == 0, k == KD - 1)
                r.then_inc(S["h_done"], 1)

            def B(b, rep, m):
                js = slice(m * MS, (m + 1) * MS)
                wait_free(eng, FM_RING, f"b{m}", b, rep, FM_FREED)
                for k in range(KD):
                    r = mm3(fm_bank(f"b{m}")[:, :], [w[:, k * NS:(k + 1) * NS] for w in b_w],
                            (xT_hi[:, js, k, :], xT_lo[:, js, k, :]), k == 0, k == KD - 1)
                r.then_inc(S["b_done"], 1)

            def SG(b, rep, m):
                wait_free(eng, FM_RING, f"s{m}", b, rep, FM_FREED)
                ps = fm_bank(f"s{m}")[:, :]
                for f in range(KF):
                    hi, lo = [w[:, f * NS:(f + 1) * NS] for w in s2_w]
                    eng.wait_ge(S["h1hi_ok"], prep_at("h1hi_ok", b + 1, KF * m + f))
                    eng.matmul(ps, hi, h1_hi[:, f, :], start=(f == 0), stop=False)
                    eng.matmul(ps, lo, h1_hi[:, f, :], start=False, stop=False)
                    eng.wait_ge(S["h1lo_ok"], prep_at("h1lo_ok", b + 1, KF * m + f))
                    r = eng.matmul(ps, hi, h1_lo[:, f, :], start=False, stop=(f == KF - 1))
                r.then_inc(S["s_done"], 1)

            def tail_and_scan(b, rep):
                a = (b, rep)
                if rep == 0:
                    G(*a, 0, {2: 0, 3: 1})
                    G(*a, 1, {0: 2, 1: 3, 2: 4, 3: 5})
                    G(*a, 2, {0: 6, 1: 7, 2: 8, 3: 9})
                    G(*a, 3, {0: 10, 1: 11})
                    return
                G(*a, 0, {2: 0, 3: 1})
                W1f(*a, 1, 0)
                scan_step(*a, 2)
                W1f(*a, 1, 1)
                scan_step(*a, 3)
                G(*a, 1, {2: 4, 3: 5})
                R(*a, 1)
                scan_step(*a, 6)
                W2(*a, 4)
                scan_step(*a, 7)
                W2(*a, 5)
                G(*a, 2, {2: 8, 3: 9})
                W2(*a, 6)
                scan_step(*a, 10)
                RT(*a, 1)
                W2(*a, 7)
                scan_step(*a, 11)
                G(*a, 3)

            def body(b, rep):
                a = (b, rep)
                prep = rep + 1 < NB
                Y(*a, 0)
                G(*a, 4)
                Y(*a, 1)
                G(*a, 5)
                if prep:
                    FT(*a, 0)
                Y(*a, 2)
                T(*a, 0)
                G(*a, 6)
                if prep:
                    FT(*a, 1)
                Y(*a, 3)
                T(*a, 1)
                G(*a, 7)
                if prep:
                    FT(*a, 2)
                Y(*a, 4)
                if prep:
                    FT(*a, 3)
                Y(*a, 5)
                T(*a, 2)
                if prep:
                    H(*a, 0, 0)
                    H(*a, 0, 1)
                T(*a, 3)
                if prep:
                    FT(*a, 4)
                    B(*a, 0)
                    SG(*a, 0)
                Y(*a, 6)
                if prep:
                    FT(*a, 5)
                W1f(*a, 0, 0)
                Y(*a, 7)
                if prep:
                    FT(*a, 6)
                if prep:
                    W1f(*a, 0, 1)
                    FT(*a, 7)
                    R(*a, 0)
                    T(*a, 4)
                    RT(*a, 0)
                    W2(*a, 0)
                    W2(*a, 1)
                    T(*a, 5)
                    W2(*a, 2)
                    H(*a, 1, 0)
                    T(*a, 6)
                    W2(*a, 3)
                    H(*a, 1, 1)
                    T(*a, 7)
                    B(*a, 1)
                    SG(*a, 1)
                else:
                    W1f(*a, 0, 1)
                    R(*a, 0)
                    T(*a, 4)
                    T(*a, 5)
                    RT(*a, 0)
                    W2(*a, 0)
                    T(*a, 6)
                    W2(*a, 1)
                    W2(*a, 2)
                    T(*a, 7)
                    W2(*a, 3)

            def parts_of(name, lo, lo_at):
                eng.wait_ge(hi_ok, HI[name])
                eng.wait_ge(lo, lo_at[name])

            a = (-1, -1)
            for i in range(6):
                power(i)
            FT(*a, 0)
            power(6)
            FT(*a, 1)
            power(7)
            FT(*a, 2)
            power(8)
            FT(*a, 3)
            power(9)
            power(10)
            parts_of("s1", lo_pool, LO_POOL)
            H(*a, 0, 0)
            power(11)
            H(*a, 0, 1)
            power(12)
            FT(*a, 4)
            power(13)
            parts_of("b", lo_dve, LO_DVE)
            B(*a, 0)
            power(14)
            FT(*a, 5)
            power(15)
            parts_of("s2", lo_dve, LO_DVE)
            SG(*a, 0)
            power(16)
            FT(*a, 6)
            power(17)
            FT(*a, 7)
            power(18)
            power(19)
            H(*a, 1, 0)
            power(20)
            H(*a, 1, 1)
            power(21)
            B(*a, 1)
            power(22)
            SG(*a, 1)
            power(23)
            assert len(POWERS) == 24
            eng.wait_ge(pw_cp, len(POWERS))
            eng.wait_ge(hi_ok, HI["g"])
            eng.wait_ge(lo_pool, LO_POOL["g"])
            eng.wait_ge(lo_dve, LO_DVE["biases"])
            tail_and_scan(0, 0)
            eng.wait_ge(w_ld["comb"], 2 * 16)
            eng.wait_ge(hi_ok, HI["r"])
            eng.wait_ge(lo_pool, LO_POOL["r"])
            body(0, 0)
            with eng.Fori(1, NB - 1) as b:
                tail_and_scan(b, 1)
                body(b, 1)
            tail_and_scan(NB - 1, NB - 1)
            body(NB - 1, NB - 1)
            for f in range(KF):
                W1f(NB, NB, 1, f)
            R(NB, NB, 1)
            RT(NB, NB, 1)
            for j in range(MS, L):
                W2(NB, NB, j)

            def routed_ffn(w1, w2):
                for f in range(KF):
                    for k in range(KD):
                        r = eng.matmul(TM[0][:, f * P:(f + 1) * P], w1[:, k, f * P:(f + 1) * P], q_xT[:, k, :],
                                       start=(k == 0), stop=(k == KD - 1))
                r.then_inc(EDGE["h"], 1)
                take(eng, "hr")
                for f in range(KF):
                    r = eng.matmul(TM[1][:, :], q_h[1][:, f, :], w2[:, f, :], start=(f == 0), stop=(f == KF - 1))
                r.then_inc(EDGE["y"], 1)
                take(eng, "acc")

            with if_routed(eng):
                take(eng, "ws_in", 48)
                with eng.Fori(0, NT) as t:
                    take(eng, "xn")
                    transposes(TR[0], q_xn).then_inc(EDGE["tr"], 1)
                    take(eng, "xt")
                    for k in range(KD):
                        r = eng.matmul(SC[:, 0:NE], q_xT[:, k, :], q_wr[:, k, :], start=(k == 0), stop=(k == KD - 1))
                    r.then_inc(EDGE["lg"], 1)
                    take(eng, "pr")
                    routed_ffn(q_s1, q_s2)
                    with eng.Fori(0, NE // 2) as e:
                        for s in range(2):
                            take(eng, f"w_in{s}", 32)
                            routed_ffn(q_w1[s], q_w2[s])
                            eng.sem_inc(EDGE["w_free"], 1)

        @block.scalar
        def _(eng):
            def high_part(name):
                load = "bias" if name in ("by", "bg") else name
                eng.wait_ge(w_ld[load], 16 * (len(BIAS_ROWS) if load == "bias" else 1))
                eng.activation(PARTS[name][0], raw[name], ACT.Copy).then_inc(hi_ok, 1)

            def copy_power(i):
                eng.wait_ge(pw_mm, i + 1)
                eng.activation(POWERS[i][0], SC[:, 0:P], ACT.Copy).then_inc(pw_cp, 1)

            def gate(b, rep, j):
                eng.wait_ge(S["g_done"], body_at("g_done", b, j))
                if j % MS == 0 and rep > 0:
                    m = j // MS
                    eng.wait_ge(S[f"out_st{m}"], body_at(f"out_st{m}", b - 1))
                elif rep == 0 and j in (0, 2, 3, 4):
                    eng.wait_ge(*{0: (lo_pool, LO_POOL["s1"]), 2: (lo_dve, LO_DVE["b"]), 3: (lo_pool, LO_POOL["c"]),
                                  4: (lo_pool, LO_POOL["f2"])}[j])
                eng.activation(work[:, j, :], tm_bank(f"g{j}")[:, :], ACT.Sigmoid).then_inc(S["gate_ok"], 1)

            def hs(b, rep, j):
                if j < L - 1:
                    eng.wait_ge(S["scan_ok"], body_at("scan_ok", b, 5 + j))
                if j >= 2:
                    eng.wait_ge(S["y_done"], body_at("y_done", b, j - 2))
                src = u[:, j, :] if j < L - 1 else carry[:, 1:P + 1]
                eng.activation(hs_hi[:, j % 2, :], src, ACT.Copy).then_inc(S["hs_hi_ok"], 1)

            def t_hi(b, rep, j):
                eng.wait_ge(S["t_done"], body_at("t_done", b, j))
                if j == 0 and rep > 0:
                    eng.wait_ge(S["r_done"], body_at("r_done", b - 1, NM - 1))
                elif j % MS == 0 and j:
                    eng.wait_ge(S["r_done"], body_at("r_done", b, j // MS - 1))
                eng.activation(x2T_hi[:, j % MS, :, :], tr_bank(f"t{j}")[:, :].rearrange("p (k n) -> p k n", n=P),
                               ACT.Copy).then_inc(S["t_hi"], 1)

            def ft_hi(b, rep, j):
                eng.wait_ge(S["ft_done"], prep_at("ft_done", b + 1, j))
                if rep >= 0:
                    eng.wait_ge(S["y_done"], body_at("y_done", b, j))
                eng.activation(xT_hi[:, j, :, :], ft_bank(rep, j)[:, :].rearrange("p (k n) -> p k n", n=P), ACT.Copy)\
                   .then_inc(S["ft_hi"], 1)

            def hidden(b, rep, m, f):
                name = f"w{m}{f}"
                i = b + shift(name)
                eng.wait_ge(S["w1_done"], body_at("w1_done", i, KF * m + f))
                wait_free(eng, HF_RING, name, b, rep, HF_FREED)
                eng.activation(hf_row(name), fm_bank(name)[:, :], ACT.Relu).then_inc(S["relu_ok"], 1)
                eng.wait_ge(S["relu_ok"], body_at("relu_ok", i, KF * m + f))
                eng.activation(hf_row(name), hf_row(name), ACT.Square).then_inc(S["sq_ok"], 1)

            def lg(b, rep, m):
                name = f"r{m}"
                eng.wait_ge(S["r_done"], body_at("r_done", b + shift(name), m))
                wait_free(eng, HF_RING, name, b, rep, HF_FREED)
                eng.activation(hf_row(name)[0:RC, :], fm_bank(name)[0:RC, :], ACT.Copy).then_inc(S["lg_ok"], 1)

            def sig(b, rep, m, f):
                name = f"h{m}{f}"
                eng.wait_ge(S["h_done"], prep_at("h_done", b + 1, KF * m + f))
                wait_free(eng, HF_RING, name, b, rep, HF_FREED)
                eng.activation(hf_row(name), fm_bank(name)[:, :], ACT.Sigmoid, bias=b_col[:, f:f + 1])\
                   .then_inc(S["sig_ok"], 1)

            def s_gate(b, rep, m):
                eng.wait_ge(S["s_done"], prep_at("s_done", b + 1, m))
                if m or rep >= 0:
                    eng.wait_ge(S["u_ok"], prep_at("u_ok", b + 1 if m else b, (m - 1) % NM))
                eng.activation(sg[:, :], fm_bank(f"s{m}")[:, :], ACT.Sigmoid, bias=b_col[:, 2:3])\
                   .then_inc(S["s_ok"], 1)

            def zn(b, rep, j):
                eng.wait_ge(S["z_nm"], body_at("z_nm", b + shift(f"z{j}"), j))
                eng.activation(work[:, j, :], z_bank(rep, j)[:, :], ACT.Identity, bias=nmz[:, j:j + 1],
                               scale=rsz[:, j:j + 1]).then_inc(S["zn_ok"], 1)

            def tail_and_scan(b, rep):
                a = (b, rep)
                tail = rep > 0
                gate(*a, 0)
                if tail:
                    hidden(*a, 1, 0)
                    hidden(*a, 1, 1)
                gate(*a, 1)
                if tail:
                    lg(*a, 1)
                    zn(*a, 4)
                gate(*a, 2)
                if tail:
                    zn(*a, 5)
                hs(*a, 0)
                hs(*a, 1)
                if tail:
                    zn(*a, 6)
                gate(*a, 3)
                if tail:
                    zn(*a, 7)

            def body(b, rep):
                a = (b, rep)
                prep = rep + 1 < NB
                hs(*a, 2)
                gate(*a, 4)
                hs(*a, 3)
                gate(*a, 5)
                if prep:
                    ft_hi(*a, 0)
                hs(*a, 4)
                t_hi(*a, 0)
                gate(*a, 6)
                if prep:
                    ft_hi(*a, 1)
                hs(*a, 5)
                t_hi(*a, 1)
                gate(*a, 7)
                if prep:
                    ft_hi(*a, 2)
                hs(*a, 6)
                if prep:
                    ft_hi(*a, 3)
                hs(*a, 7)
                t_hi(*a, 2)
                if prep:
                    sig(*a, 0, 0)
                    sig(*a, 0, 1)
                t_hi(*a, 3)
                if prep:
                    ft_hi(*a, 4)
                    s_gate(*a, 0)
                    ft_hi(*a, 5)
                hidden(*a, 0, 0)
                if prep:
                    ft_hi(*a, 6)
                    hidden(*a, 0, 1)
                    ft_hi(*a, 7)
                    lg(*a, 0)
                    t_hi(*a, 4)
                    zn(*a, 0)
                    t_hi(*a, 5)
                    zn(*a, 1)
                    sig(*a, 1, 0)
                    t_hi(*a, 6)
                    zn(*a, 2)
                    sig(*a, 1, 1)
                    zn(*a, 3)
                    t_hi(*a, 7)
                    s_gate(*a, 1)
                else:
                    hidden(*a, 0, 1)
                    lg(*a, 0)
                    t_hi(*a, 4)
                    t_hi(*a, 5)
                    t_hi(*a, 6)
                    zn(*a, 0)
                    t_hi(*a, 7)
                    zn(*a, 1)
                    zn(*a, 2)

            eng.wait_ge(lo_pool, LO_POOL["constants"])
            eng.activation(first_sigmoid[:, :], negh[:, 0:1], ACT.Sigmoid)
            a = (-1, -1)
            for i in range(5):
                copy_power(i)
            high_part("s1")
            copy_power(5)
            for j in range(MS):
                ft_hi(*a, j)
                copy_power(6 + j)
            copy_power(10)
            high_part("b")
            high_part("s2")
            high_part("by")
            high_part("bg")
            high_part("g")
            eng.wait_ge(w_ld["small"], 3 * 16)
            sig(*a, 0, 0)
            copy_power(11)
            sig(*a, 0, 1)
            copy_power(12)
            ft_hi(*a, 4)
            copy_power(13)
            high_part("d")
            copy_power(14)
            ft_hi(*a, 5)
            copy_power(15)
            eng.wait_ge(lo_dve, LO_DVE["biases"])
            s_gate(*a, 0)
            copy_power(16)
            ft_hi(*a, 6)
            copy_power(17)
            ft_hi(*a, 7)
            copy_power(18)
            copy_power(19)
            sig(*a, 1, 0)
            copy_power(20)
            high_part("c")
            high_part("f1")
            sig(*a, 1, 1)
            copy_power(21)
            high_part("f2")
            copy_power(22)
            s_gate(*a, 1)
            copy_power(23)
            high_part("r")
            tail_and_scan(0, 0)
            body(0, 0)
            with eng.Fori(1, NB - 1) as b:
                tail_and_scan(b, 1)
                body(b, 1)
            tail_and_scan(NB - 1, NB - 1)
            body(NB - 1, NB - 1)
            hidden(NB, NB, 1, 0)
            zn(NB - 1, NB - 1, 3)
            hidden(NB, NB, 1, 1)
            lg(NB, NB, 1)
            eng.wait_ge(S["top_ok"], body_at("top_ok", NB - 1, NM - 1))
            eng.wait_ge(diffs_ok, 1)
            eng.activation(dif[:, :], dif[:, :], ACT.Exp).then_inc(exp_ok, 1)
            for j in range(MS, L):
                zn(NB, NB, j)

            def routed_ffn():
                take(eng, "h")
                h = TM[0][:, 0:FH].rearrange("p (f n) -> p f n", n=P)
                eng.activation(q_h[0], h, ACT.Relu).then_inc(EDGE["hr1"], 1)
                take(eng, "hr1")
                eng.activation(q_h[1], q_h[0], ACT.Square).then_inc(EDGE["hr"], 1)

            with if_routed(eng):
                with eng.Fori(0, NT) as t:
                    take(eng, "tr")
                    eng.activation(q_xT, TR[0][:, :].rearrange("p (k n) -> p k n", n=P), ACT.Copy)\
                       .then_inc(EDGE["xt"], 1)
                    take(eng, "d")
                    eng.activation(q_d, q_d, ACT.Exp).then_inc(EDGE["e"], 1)
                    routed_ffn()
                    with eng.Fori(0, NE) as e:
                        routed_ffn()

        @block.vector
        def _(eng):
            def link(ins):
                ins.then_inc(chain, 1)
                eng.wait_ge(chain, 1)
                eng.sem_inc(chain, -1)

            def stats(src, i, mv):
                link(eng.bn_stats(st6[:, i, :], src))
                link(eng.bn_aggr(mv, st6[:, i, :]))

            def ln1_stats(n, j):
                if j % MS == 0:
                    eng.wait_ge(S[f"xin_ld{j // MS}"], prep_at(f"xin_ld{j // MS}", n))
                stats(xin[:, j, :], 0, mv1[:, j, :])
                if j % MS == MS - 1:
                    m = j // MS
                    js = slice(m * MS, (m + 1) * MS)
                    eng.tensor_scalar(ve1[:, js], mv1[:, js, 1], EPS, None, ALU.add).then_inc(S["l1_var"], 1)

            def ln1_norm(n, j):
                eng.wait_ge(S["l1_rs"], prep_at("l1_rs", n, j // MS))
                eng.tensor_scalar(xin[:, j, :], xin[:, j, :], mv1[:, j, 0:1], rs1[:, j:j + 1],
                                  ALU.subtract, ALU.mult).then_inc(S["xn_ok"], 1)

            def scan_add(b, rep, i):
                eng.wait_ge(S["scan_done"], body_at("scan_done", b, i))
                if i == 0:
                    if rep > 0:
                        eng.wait_ge(S["hs_hi_ok"], body_at("hs_hi_ok", b - 1, L - 1))
                    r = eng.tensor_tensor(carry[:, 1:P + 1], SC[:, 0:P], u[:, L - 1, :], ALU.add)
                elif i <= 4:
                    s = 4 ** (i - 1)
                    r = eng.tensor_tensor(carry[:, 1 + s:P + 1], SC[:, s:P], carry[:, 1 + s:P + 1], ALU.add)
                else:
                    j = i - 5
                    r = eng.tensor_tensor(u[:, j, :], SC[:, 0:P], u[:, j, :], ALU.add)
                r.then_inc(S["scan_ok"], 1)

            def hs_low(b, rep, j):
                eng.wait_ge(S["hs_hi_ok"], body_at("hs_hi_ok", b, j))
                src = u[:, j, :] if j < L - 1 else carry[:, 1:P + 1]
                eng.tensor_tensor(hs_lo[:, j % 2, :], src, hs_hi[:, j % 2, :].bitcast(F32), ALU.subtract)\
                   .then_inc(S["hs_lo_ok"], 1)

            def attn(b, rep, j):
                eng.wait_ge(S["y_done"], body_at("y_done", b, j))
                eng.wait_ge(S["gate_ok"], body_at("gate_ok", b, j))
                eng.tensor_tensor(work[:, j, :], tm_bank(f"y{j}")[:, :], work[:, j, :], ALU.mult)\
                   .then_inc(S["v_ok"], 1)
                eng.wait_ge(S["v_ok"], body_at("v_ok", b, j))
                stats(work[:, j, :], 1, mvv[:, j, :])
                eng.tensor_scalar(rsv[:, j:j + 1], mvv[:, j, 1:2], EPS, None, ALU.add).then_inc(S["v_var"], 1)

            def attn_norm(b, rep, j):
                eng.wait_ge(S["v_rs"], body_at("v_rs", b, j))
                eng.tensor_scalar(work[:, j, :], work[:, j, :], mvv[:, j, 0:1], rsv[:, j:j + 1],
                                  ALU.subtract, ALU.mult).then_inc(S["vn_ok"], 1)

            def x1_stats(b, rep, j):
                eng.wait_ge(S["x1_ok"], body_at("x1_ok", b, j))
                stats(xres[:, j, :], 2, mvx[:, j, :])
                eng.tensor_scalar(rsx[:, j:j + 1], mvx[:, j, 1:2], EPS, None, ALU.add).then_inc(S["x1_var"], 1)

            def x1_norm(b, rep, j):
                eng.wait_ge(S["x1_rs"], body_at("x1_rs", b, j))
                eng.tensor_scalar(work[:, j, :], xres[:, j, :], mvx[:, j, 0:1], rsx[:, j:j + 1],
                                  ALU.subtract, ALU.mult).then_inc(S["xn2_ok"], 1)

            def low_of(dst, bank, hi):
                return eng.tensor_tensor(dst, bank[:, :].rearrange("p (k n) -> p k n", n=P), hi.bitcast(F32),
                                         ALU.subtract)

            def t_low(b, rep, j):
                eng.wait_ge(S["t_hi"], body_at("t_hi", b, j))
                low_of(x2T_lo[:, j % MS, :, :], tr_bank(f"t{j}"), x2T_hi[:, j % MS, :, :]).then_inc(S["t_lo"], 1)

            def ft_low(b, rep, j):
                eng.wait_ge(S["ft_hi"], prep_at("ft_hi", b + 1, j))
                low_of(xT_lo[:, j, :, :], ft_bank(rep, j), xT_hi[:, j, :, :]).then_inc(S["ft_lo"], 1)

            def h1(b, rep, m, f):
                name, i = f"h{m}{f}", KF * m + f
                h = hf_row(name)
                eng.wait_ge(S["sig_ok"], prep_at("sig_ok", b + 1, i))
                eng.scalar_tensor_tensor(out=h, in0=fm_bank(name)[:, :], scalar=b_col[:, f:f + 1], in1=h,
                                         op0=ALU.add, op1=ALU.mult).then_inc(S["h1_ok"], 1)
                eng.wait_ge(S["h1_ok"], prep_at("h1_ok", b + 1, i))
                if m or rep >= 0:
                    eng.wait_ge(S["s_done"], prep_at("s_done", b + 1 if m else b, (m - 1) % NM))
                eng.tensor_copy(h1_hi[:, f, :], h).then_inc(S["h1hi_ok"], 1)

            def u_of(b, rep, m):
                eng.wait_ge(S["s_ok"], prep_at("s_ok", b + 1, m))
                eng.wait_ge(S["b_done"], prep_at("b_done", b + 1, m))
                if rep >= 0:
                    eng.wait_ge(S["hs_hi_ok"], body_at("hs_hi_ok", b, min(m * MS + MS - 1, L - 2)))
                js = slice(m * MS, (m + 1) * MS)
                eng.scalar_tensor_tensor(out=u[:, js, :].rearrange("p a b -> p (a b)"), in0=fm_bank(f"b{m}")[:, :],
                                         scalar=b_col[:, 3:4], in1=sg[:, :], op0=ALU.add, op1=ALU.mult)\
                   .then_inc(S["u_ok"], 1)

            def h2(b, rep, m, f):
                name = f"w{m}{f}"
                i = b + shift(name)
                eng.wait_ge(S["sq_ok"], body_at("sq_ok", i, KF * m + f))
                if m:
                    eng.wait_ge(S["w2_done"], body_at("w2_done", i, m * MS - 1))
                elif rep > 0:
                    eng.wait_ge(S["w2_done"], body_at("w2_done", i - 1, L - 1))
                eng.tensor_copy(h2_hi[:, f, :], hf_row(name)).then_inc(S["h2hi_ok"], 1)

            def top(b, rep, m):
                i = b + shift(f"r{m}")
                eng.wait_ge(S["rt_done"], body_at("rt_done", i, m))
                link(eng.tensor_copy(lgt[:, :], fm_bank(f"r{m}")[:, 0:MS * NE]))
                for s in range(MS):
                    r = eng.max(mx8[:, s, :], lgt[:, s * NE:(s + 1) * NE])
                r.then_inc(S["top_ok"], 1)
                eng.wait_ge(S["top_ok"], body_at("top_ok", i, m))
                link(eng.tensor_tensor(dif[:, bass.ds(i * L + m * MS, MS)], mx8[:, :, 1], mx8[:, :, 0], ALU.subtract))

            def z_stats(b, rep, j):
                i = b + shift(f"z{j}")
                eng.wait_ge(S["w2_done"], body_at("w2_done", i, j))
                stats(z_bank(rep, j)[:, :], 3, mvz[:, j, :])
                eng.tensor_scalar(rsz[:, j:j + 1], mvz[:, j, 1:2], EPS, None, ALU.add).then_inc(S["z_var"], 1)

            def z_shift(b, rep, j):
                i = b + shift(f"z{j}")
                eng.wait_ge(S["z_rs"], body_at("z_rs", i, j))
                eng.scalar_tensor_tensor(out=nmz[:, j:j + 1], in0=mvz[:, j, 0:1], scalar=-1.0, in1=rsz[:, j:j + 1],
                                         op0=ALU.mult, op1=ALU.mult).then_inc(S["z_nm"], 1)

            def tail_and_scan(b, rep):
                a = (b, rep)
                tail, prep = rep > 0, rep + 1 < NB
                scan_add(*a, 0)
                scan_add(*a, 1)
                scan_add(*a, 2)
                if tail:
                    h2(*a, 1, 0)
                if prep:
                    ln1_stats(b + 1, 0)
                scan_add(*a, 3)
                if prep:
                    ln1_stats(b + 1, 1)
                scan_add(*a, 4)
                if tail:
                    h2(*a, 1, 1)
                scan_add(*a, 5)
                if prep:
                    ln1_stats(b + 1, 2)
                scan_add(*a, 6)
                if prep:
                    ln1_stats(b + 1, 3)
                scan_add(*a, 7)
                if tail:
                    z_stats(*a, 4)
                if prep:
                    ln1_stats(b + 1, 4)
                if tail:
                    z_shift(*a, 4)
                scan_add(*a, 8)
                if tail:
                    z_stats(*a, 5)
                scan_add(*a, 9)
                if tail:
                    z_shift(*a, 5)
                scan_add(*a, 10)
                hs_low(*a, 0)
                if tail:
                    z_stats(*a, 6)
                scan_add(*a, 11)
                hs_low(*a, 1)
                if prep:
                    ln1_stats(b + 1, 5)
                if tail:
                    z_shift(*a, 6)
                    z_stats(*a, 7)
                if prep:
                    ln1_stats(b + 1, 6)
                if tail:
                    z_shift(*a, 7)
                if prep:
                    ln1_stats(b + 1, 7)
                if tail:
                    top(*a, 1)
                if prep:
                    for j in range(MS):
                        ln1_norm(b + 1, j)

            def body(b, rep):
                a = (b, rep)
                prep = rep + 1 < NB
                attn(*a, 0)
                hs_low(*a, 2)
                attn_norm(*a, 0)
                attn(*a, 1)
                hs_low(*a, 3)
                x1_stats(*a, 0)
                attn_norm(*a, 1)
                x1_norm(*a, 0)
                if prep:
                    ft_low(*a, 0)
                attn(*a, 2)
                hs_low(*a, 4)
                x1_stats(*a, 1)
                attn_norm(*a, 2)
                x1_norm(*a, 1)
                t_low(*a, 0)
                if prep:
                    ln1_norm(b + 1, 4)
                    ft_low(*a, 1)
                attn(*a, 3)
                hs_low(*a, 5)
                x1_stats(*a, 2)
                attn_norm(*a, 3)
                x1_norm(*a, 2)
                t_low(*a, 1)
                if prep:
                    ln1_norm(b + 1, 5)
                    ft_low(*a, 2)
                attn(*a, 4)
                hs_low(*a, 6)
                if prep:
                    ft_low(*a, 3)
                x1_stats(*a, 3)
                attn_norm(*a, 4)
                x1_norm(*a, 3)
                if prep:
                    ln1_norm(b + 1, 6)
                attn(*a, 5)
                hs_low(*a, 7)
                t_low(*a, 2)
                if prep:
                    h1(*a, 0, 0)
                x1_stats(*a, 4)
                if prep:
                    h1(*a, 0, 1)
                attn_norm(*a, 5)
                x1_norm(*a, 4)
                if prep:
                    ln1_norm(b + 1, 7)
                t_low(*a, 3)
                if prep:
                    ft_low(*a, 4)
                    u_of(*a, 0)
                attn(*a, 6)
                x1_stats(*a, 5)
                attn_norm(*a, 6)
                x1_norm(*a, 5)
                if prep:
                    ft_low(*a, 5)
                h2(*a, 0, 0)
                attn(*a, 7)
                if prep:
                    ft_low(*a, 6)
                x1_stats(*a, 6)
                h2(*a, 0, 1)
                attn_norm(*a, 7)
                x1_norm(*a, 6)
                if prep:
                    ft_low(*a, 7)
                if prep:
                    x1_stats(*a, 7)
                    t_low(*a, 4)
                    z_stats(*a, 0)
                    z_stats(*a, 1)
                    z_shift(*a, 0)
                    x1_norm(*a, 7)
                    z_shift(*a, 1)
                    t_low(*a, 5)
                    top(*a, 0)
                    h1(*a, 1, 0)
                    z_stats(*a, 2)
                    t_low(*a, 6)
                    z_shift(*a, 2)
                    z_stats(*a, 3)
                    h1(*a, 1, 1)
                    z_shift(*a, 3)
                    t_low(*a, 7)
                    u_of(*a, 1)
                else:
                    t_low(*a, 4)
                    x1_stats(*a, 7)
                    t_low(*a, 5)
                    x1_norm(*a, 7)
                    z_stats(*a, 0)
                    t_low(*a, 6)
                    z_shift(*a, 0)
                    z_stats(*a, 1)
                    t_low(*a, 7)
                    z_shift(*a, 1)
                    top(*a, 0)
                    z_stats(*a, 2)
                    z_shift(*a, 2)
                    z_stats(*a, 3)

            eng.memset(carry[:, 0:1], 0.0)
            eng.memset(flag[:, 0:1], 0.0)
            eng.memset(ones2[:, :].bitcast(F32), 1.0).then_inc(lo_dve, 1)
            a = (-1, -1)
            for j in range(MS):
                ln1_stats(0, j)
            for j in range(MS):
                ln1_norm(0, j)
            ft_low(*a, 0)
            ft_low(*a, 1)
            ln1_stats(0, 4)
            ft_low(*a, 2)
            ft_low(*a, 3)
            ln1_stats(0, 5)
            ln1_stats(0, 6)
            ln1_stats(0, 7)
            low_part(eng, "b").then_inc(lo_dve, 1)
            low_part(eng, "s2").then_inc(lo_dve, 1)
            eng.wait_ge(w_ld["small"], 3 * 16)
            h1(*a, 0, 0)
            ln1_norm(0, 4)
            h1(*a, 0, 1)
            for j in range(MS + 1, L):
                ln1_norm(0, j)
            ft_low(*a, 4)
            eng.wait_ge(hi_ok, HI["bg"])
            for row, _, raw_row in BIAS_ROWS:
                if row % 64:
                    dst = (bias_y if raw_row is brow else bias_g)[row:row + 1, :]
                    r = eng.tensor_tensor(dst, raw_row[row:row + 1, :], dst.bitcast(F32), ALU.subtract)
            r.then_inc(lo_dve, 1)
            ft_low(*a, 5)
            u_of(*a, 0)
            ft_low(*a, 6)
            ft_low(*a, 7)
            h1(*a, 1, 0)
            h1(*a, 1, 1)
            eng.wait_ge(pw_mm, 23)
            u_of(*a, 1)
            tail_and_scan(0, 0)
            eng.wait_ge(lo_pool, LO_POOL["r"])
            body(0, 0)
            with eng.Fori(1, NB - 1) as b:
                tail_and_scan(b, 1)
                body(b, 1)
            tail_and_scan(NB - 1, NB - 1)
            body(NB - 1, NB - 1)
            h2(NB, NB, 1, 0)
            z_shift(NB - 1, NB - 1, 3)
            h2(NB, NB, 1, 1)
            top(NB, NB, 1)
            eng.memset(flag[:, 1:2], 0.0).then_inc(diffs_ok, 1)
            for j in range(MS, L):
                z_stats(NB, NB, j)
                if j > MS:
                    z_shift(NB, NB, j - 1)
            eng.wait_ge(exp_ok, 1)
            eng.tensor_scalar(dif[:, :], dif[:, :], 1.0, None, ALU.add).then_inc(flag_dve, 1)
            eng.wait_ge(flag_dve, 1)
            eng.reciprocal(dif[:, :], dif[:, :]).then_inc(flag_dve, 1)
            eng.wait_ge(flag_dve, 2)
            eng.tensor_scalar(dif[:, :], dif[:, :], 1.0, None, ALU.is_ge).then_inc(flag_dve, 1)
            eng.wait_ge(flag_dve, 3)
            eng.tensor_reduce(flag[:, 0:1], dif[:, :], AX.X, ALU.max).then_inc(flag_dve, 1)
            z_shift(NB, NB, L - 1)
            for j in (L - 2, L - 1):
                eng.wait_ge(S["zn_ok"], body_at("zn_ok", NB - 1, j))
                eng.tensor_tensor(work[:, j, :], work[:, j, :], xres[:, j, :], ALU.add).then_inc(last_out, 1)
            eng.wait_ge(flag_pool, 1)
            eng.tensor_copy(flag_i[:, :], flag[:, 1:2]).then_inc(flag_ok, 1)

            def routed_norm(dst, src):
                link(eng.bn_stats(st6[:, 0, :], src))
                link(eng.bn_aggr(q_mv, st6[:, 0, :]))
                eng.tensor_scalar(q_rs, q_mv[:, 1:2], EPS, None, ALU.add).then_inc(EDGE["var"], 1)
                take(eng, "rs")
                return eng.tensor_scalar(dst, src, q_mv[:, 0:1], q_rs, ALU.subtract, ALU.mult)

            with if_routed(eng):
                with eng.Fori(0, NT) as t:
                    take(eng, "x_in", 16)
                    routed_norm(q_xn, q_x1).then_inc(EDGE["xn"], 1)
                    take(eng, "lg")
                    link(eng.tensor_copy(q_lg, SC[:, 0:NE]))
                    link(eng.max(q_mx, q_lg))
                    eng.tensor_tensor(q_d, q_mx[:, 1:2], q_mx[:, 0:1], ALU.subtract).then_inc(EDGE["d"], 1)
                    take(eng, "e")
                    link(eng.tensor_scalar(q_d, q_d, 1.0, None, ALU.add))
                    link(eng.reciprocal(q_d, q_d))
                    link(eng.tensor_scalar(q_d, q_d, 1.0, None, ALU.is_ge))
                    link(eng.tensor_scalar(q_pr, q_lg, q_mx[:, 0:1], q_d, ALU.is_equal, ALU.mult))
                    eng.memset(flag[:, 2:3], 0.0).then_inc(EDGE["pr"], 1)
                    take(eng, "y")
                    link(eng.tensor_copy(q_acc, TM[1][:, :]))
                    eng.sem_inc(EDGE["acc"], 1)
                    with eng.Fori(0, NE) as e:
                        take(eng, "y")
                        link(eng.scalar_tensor_tensor(out=q_acc, in0=TM[1][:, :], scalar=q_pr[:, bass.ds(e, 1)],
                                                      in1=q_acc, op0=ALU.mult, op1=ALU.add))
                        eng.sem_inc(EDGE["acc"], 1)
                    link(routed_norm(q_xn, q_acc))
                    eng.tensor_tensor(q_o, q_xn, q_x1, ALU.add).then_inc(EDGE["o_ok"], 1)

        @block.gpsimd
        def _(eng):
            eng.memset(brow, 0.0)
            eng.memset(grow, 0.0)
            eng.memset(negh[:, :], -0.5).then_inc(lo_pool, 1)
            eng.wait_ge(lo_pool, LO_POOL["constants"])

            def power(dst, src, n):
                return eng.tensor_tensor(dst, src, negh[:, 0:n], ALU.pow)

            def ln1_rs(n, m):
                eng.wait_ge(S["l1_var"], prep_at("l1_var", n, m))
                js = slice(m * MS, (m + 1) * MS)
                power(rs1[:, js], ve1[:, js], MS).then_inc(S["l1_rs"], 1)

            def v_rs(b, j):
                eng.wait_ge(S["v_var"], body_at("v_var", b, j))
                power(rsv[:, j:j + 1], rsv[:, j:j + 1], 1).then_inc(S["v_rs"], 1)

            def x1_rs(b, j):
                eng.wait_ge(S["x1_var"], body_at("x1_var", b, j))
                power(rsx[:, j:j + 1], rsx[:, j:j + 1], 1).then_inc(S["x1_rs"], 1)

            def z_rs(b, j):
                eng.wait_ge(S["z_var"], body_at("z_var", b, j))
                power(rsz[:, j:j + 1], rsz[:, j:j + 1], 1).then_inc(S["z_rs"], 1)

            def x1(b, j):
                if j % MS == 0:
                    m = j // MS
                    eng.wait_ge(S[f"xres_ld{m}"], body_at(f"xres_ld{m}", b))
                eng.wait_ge(S["vn_ok"], body_at("vn_ok", b, j))
                eng.tensor_tensor(xres[:, j, :], work[:, j, :], xres[:, j, :], ALU.add).then_inc(S["x1_ok"], 1)

            def outs(b, j):
                eng.wait_ge(S["zn_ok"], body_at("zn_ok", b, j))
                eng.tensor_tensor(work[:, j, :], work[:, j, :], xres[:, j, :], ALU.add).then_inc(S["out_ok"], 1)

            def h1_low(n, m, f):
                name, i = f"h{m}{f}", KF * m + f
                eng.wait_ge(S["h1hi_ok"], prep_at("h1hi_ok", n, i))
                eng.tensor_tensor(h1_lo[:, f, :], hf_row(name), h1_hi[:, f, :].bitcast(F32),
                                  ALU.subtract).then_inc(S["h1lo_ok"], 1)

            def h2_low(b, m, f):
                name, i = f"w{m}{f}", KF * m + f
                eng.wait_ge(S["h2hi_ok"], body_at("h2hi_ok", b, i))
                eng.tensor_tensor(h2_lo[:, f, :], hf_row(name), h2_hi[:, f, :].bitcast(F32),
                                  ALU.subtract).then_inc(S["h2lo_ok"], 1)

            def tail(b, ln1):
                h2_low(b, 1, 0)
                h2_low(b, 1, 1)
                if ln1 is None and b == NB - 1:
                    outs(b, 3)
                z_rs(b, 4)
                z_rs(b, 5)
                outs(b, 4)
                z_rs(b, 6)
                if ln1 is not None:
                    ln1_rs(ln1, 0)
                outs(b, 5)
                z_rs(b, 7)
                if ln1 is not None or b == NB - 2:
                    outs(b, 6)
                    outs(b, 7)
                if ln1 is not None:
                    ln1_rs(ln1, 1)

            def body(b, rep):
                prep = rep + 1 < NB
                v_rs(b, 0)
                x1(b, 0)
                for j in range(1, L):
                    v_rs(b, j)
                    if j == 5 and prep:
                        h1_low(b + 1, 0, 0)
                    x1_rs(b, j - 1)
                    if j == 5 and prep:
                        h1_low(b + 1, 0, 1)
                    if j == 7:
                        h2_low(b, 0, 1)
                    x1(b, j)
                    if j == 6:
                        h2_low(b, 0, 0)
                x1_rs(b, 7)
                z_rs(b, 0)
                z_rs(b, 1)
                outs(b, 0)
                if prep:
                    h1_low(b + 1, 1, 0)
                z_rs(b, 2)
                outs(b, 1)
                outs(b, 2)
                z_rs(b, 3)
                if prep:
                    h1_low(b + 1, 1, 1)
                    outs(b, 3)

            ln1_rs(0, 0)
            low_part(eng, "s1").then_inc(lo_pool, 1)
            ln1_rs(0, 1)
            h1_low(0, 0, 0)
            h1_low(0, 0, 1)
            low_part(eng, "g").then_inc(lo_pool, 1)
            h1_low(0, 1, 0)
            h1_low(0, 1, 1)
            for name in ("d", "c", "f1", "f2", "r"):
                low_part(eng, name).then_inc(lo_pool, 1)
            ln1_rs(1, 0)
            ln1_rs(1, 1)
            body(0, 0)
            with eng.Fori(1, NB - 1) as b:
                tail(b - 1, b + 1)
                body(b, 1)
            tail(NB - 2, None)
            body(NB - 1, NB - 1)
            tail(NB - 1, None)
            eng.wait_ge(flag_dve, 4)
            eng.partition_all_reduce(flag[:, 1:2], flag[:, 0:1], P, bass.bass_isa.ReduceOp.max).then_inc(flag_pool, 1)

            with if_routed(eng):
                with eng.Fori(0, 2 * NT) as t:
                    take(eng, "var")
                    power(q_rs, q_rs, 1).then_inc(EDGE["rs"], 1)


def kernel(**inputs):
    import numpy as np
    import concourse.bacc as bacc
    from concourse.bass_utils import run_bass_kernel_spmd

    nc = bacc.Bacc("TRN2", target_bir_lowering=False, num_devices=1)
    a = {k.replace("L0_attn_", "").replace("L0_ffn_", ""): np.asarray(v) for k, v in inputs.items()}
    names = ["x", "A", ("A", 1), ("B_w", 1), "B_b", ("C_w", 1), "C_b", ("D_w", 1), "D_b", ("s_w1", 1), "s_b1",
             ("s_w2", 1), "s_b2", ("g_w", 1), "g_b", "Ws1", "Ws2", "W1", "W2", "Wr"]
    arrays, args = {}, []

    def give(name, array):
        array = np.ascontiguousarray(array)
        arrays[name] = array
        args.append(nc.dram_tensor(name, array.shape, mybir.dt.from_np(array.dtype), kind="ExternalInput").ap())

    for n in names:
        if isinstance(n, tuple):
            give(f"in_{n[0]}_t", a[n[0]].T)
        else:
            give(f"in_{n}", a[n])
    give("in_eye", np.eye(P, dtype=np.float32))
    out = nc.dram_tensor("out_0", a["x"].shape, F32, kind="ExternalOutput").ap()
    build(nc, *args, out)
    r = run_bass_kernel_spmd(nc, [arrays], core_ids=[0])
    return r.results[0]["out_0"]
```
